# Optimizing a Trainium2 kernel written in Bass

```python
import numpy as np
import jax
import jax.numpy as jnp

def _softmax(x, axis=-1):
    return jax.nn.softmax(x, axis=axis)

def _gelu(x):
    return jax.nn.gelu(x, approximate=True)

def _silu(x):
    return jax.nn.silu(x)

def _sigmoid(x):
    return jax.nn.sigmoid(x)

def _layernorm(x, axis=-1, eps=1e-05):
    m = jnp.mean(x, axis=axis, keepdims=True)
    v = jnp.var(x, axis=axis, keepdims=True)
    return (x - m) / jnp.sqrt(v + eps)

def _scatter_add(tgt, idx, src, axis=0):
    return tgt.at[idx].add(src)

def _segment_sum(src, seg, n):
    return jax.ops.segment_sum(src, seg, n)
kernel_name = 'mk_adj_resnorm_d4_adj_r2_c87d3d'

def setup_inputs(seed: int=0):
    np.random.seed(seed)
    _w = jnp.asarray

    def _rec_inputs():
        import jax
        import jax.numpy as jnp
        _gk = jax.random.key(seed)
        x = -0.0001538 + 1 * jax.random.normal(jax.random.fold_in(_gk, 1), (128, 64, 384), jnp.float32)
        _w = (1.0 + jnp.arange(64, dtype=jnp.float32)) ** (-0.5)
        _w = _w / _w.mean()
        _pij = jnp.clip(0.0625 * _w[:, None] * _w[None, :], 0.0, 1.0)
        _a = jax.random.uniform(jax.random.fold_in(_gk, 2), (128, 64, 64)) < _pij
        _a = jnp.logical_or(_a, jnp.swapaxes(_a, -1, -2))
        _a = jnp.logical_or(_a, jnp.eye(64, dtype=bool))
        _af = _a.astype(jnp.float32)
        _af = _af * jax.random.uniform(jax.random.fold_in(_gk, 3), (128, 64, 64), jnp.float32, 0.05, 4.42607)
        adj = _af
        return (x, adj)
    x, adj = _rec_inputs()

    def _L0_gnn_setup():
        import jax, jax.numpy as jnp
        import numpy as np
        NUM_HEADS = 12
        HIDDEN = 384
        HEAD = HIDDEN // NUM_HEADS
        B, N = (16, 256)
        key = jax.random.key(seed)
        ks = jax.random.split(key, 9)
        s = 0.02
        return {'x': jax.random.normal(ks[0], (B, N, HIDDEN), jnp.float32), 'spatial_encoding': jax.random.normal(ks[1], (B, N, N), jnp.float32), 'edge_encoding': jax.random.normal(ks[2], (B, N, N), jnp.float32), 'Wq': jax.random.normal(ks[3], (HIDDEN, HIDDEN), jnp.float32) * s, 'Wk': jax.random.normal(ks[4], (HIDDEN, HIDDEN), jnp.float32) * s, 'Wv': jax.random.normal(ks[5], (HIDDEN, HIDDEN), jnp.float32) * s, 'bv': jax.random.normal(ks[6], (HIDDEN,), jnp.float32) * s, 'Wo': jax.random.normal(ks[7], (HIDDEN, HIDDEN), jnp.float32) * s, 'bo': jax.random.normal(ks[8], (HIDDEN,), jnp.float32) * s}
    _L0_gnn_all = _L0_gnn_setup()
    _L0_gnn_in = {k: v for k, v in _L0_gnn_all.items() if k in ('Wq', 'Wk', 'Wv', 'bv', 'Wo', 'bo')}
    del _L0_gnn_all

    def _L1_gnn_setup():
        import jax, jax.numpy as jnp
        import numpy as np
        B, N, D, H = (8, 512, 384, 12)
        HD = D // H

        def _split_heads(x):
            b, n, _ = x.shape
            return x.reshape(b, n, H, HD).transpose(0, 2, 1, 3)
        key = jax.random.key(seed)
        ks = jax.random.split(key, 10)
        input_graph = jax.random.normal(ks[0], (B, N, D), dtype=jnp.float32)
        u = jax.random.uniform(ks[1], (B, N, N), dtype=jnp.float32)
        keep = jax.random.uniform(ks[2], (B, N, N)) < 0.15
        adj = jnp.where(keep, u, 0.0)
        s = 1.0 / np.sqrt(D)
        Wq = jax.random.normal(ks[3], (D, D), dtype=jnp.float32) * s
        bq = jnp.zeros((D,), dtype=jnp.float32)
        Wk = jax.random.normal(ks[4], (D, D), dtype=jnp.float32) * s
        bk = jnp.zeros((D,), dtype=jnp.float32)
        Wv = jax.random.normal(ks[5], (D, D), dtype=jnp.float32) * s
        bv = jnp.zeros((D,), dtype=jnp.float32)
        beta = jnp.asarray(0.1, dtype=jnp.float32)
        return {'input_graph': input_graph, 'adj': adj, 'Wq': Wq, 'bq': bq, 'Wk': Wk, 'bk': bk, 'Wv': Wv, 'bv': bv, 'beta': beta}
    _L1_gnn_all = _L1_gnn_setup()
    _L1_gnn_in = {k: v for k, v in _L1_gnn_all.items() if k in ('Wq', 'bq', 'Wk', 'bk', 'Wv', 'bv', 'beta')}
    del _L1_gnn_all

    def _L2_gnn_setup():
        import jax, jax.numpy as jnp
        import numpy as np
        LN_EPS = 1e-12

        def _digcn_forward(hidden_state, adjacency_matrix, Wl, bl, Ws, bs, Wr, br, ln_w, ln_b):
            B, S, D = hidden_state.shape
            temper = jnp.asarray(D, jnp.float32) ** 0.5
            i = jnp.arange(S)
            upper = (i[None, :] > i[:, None]).astype(hidden_state.dtype)
            lower = (i[None, :] < i[:, None]).astype(hidden_state.dtype)

            def layer(h, params):
                wl, b_l, ws, b_s, wr, b_r, g, beta = params
                u = jnp.einsum('bid,bjd->bij', h, h) / temper
                a = jax.nn.softmax(u, axis=-1)
                delta = a * adjacency_matrix
                attn = delta / (jnp.sum(delta, axis=-1, keepdims=True) + 1e-10)
                hl = h @ wl.T + b_l
                hs = h @ ws.T + b_s
                hr = h @ wr.T + b_r
                diag_a = jnp.diagonal(attn, axis1=1, axis2=2)
                ctx = jnp.einsum('bij,bjd->bid', attn * upper, hl) + diag_a[..., None] * hs + jnp.einsum('bij,bjd->bid', attn * lower, hr)
                mean = ctx.mean(-1, keepdims=True)
                var = ctx.var(-1, keepdims=True)
                o = (ctx - mean) / jnp.sqrt(var + LN_EPS) * g + beta
                return (jax.nn.relu(o), None)
            out, _ = jax.lax.scan(layer, hidden_state, (Wl, bl, Ws, bs, Wr, br, ln_w, ln_b))
            return out
        key = jax.random.key(seed)
        ks = jax.random.split(key, 6)
        B, S, D, L = (8, 512, 384, 2)
        scale = (1.0 / D) ** 0.5
        hidden_state = jax.random.normal(ks[0], (B, S, D), jnp.float32)
        adjacency_matrix = (jax.random.uniform(ks[1], (B, S, S)) < 0.05).astype(jnp.float32)
        Wl = jax.random.normal(ks[2], (L, D, D), jnp.float32) * scale
        Ws = jax.random.normal(ks[3], (L, D, D), jnp.float32) * scale
        Wr = jax.random.normal(ks[4], (L, D, D), jnp.float32) * scale
        bl = jnp.zeros((L, D), jnp.float32)
        bs = jnp.zeros((L, D), jnp.float32)
        br = jnp.zeros((L, D), jnp.float32)
        ln_w = jnp.ones((L, D), jnp.float32)
        ln_b = jnp.zeros((L, D), jnp.float32)
        return dict(hidden_state=hidden_state, adjacency_matrix=adjacency_matrix, Wl=Wl, bl=bl, Ws=Ws, bs=bs, Wr=Wr, br=br, ln_w=ln_w, ln_b=ln_b)
    _L2_gnn_all = _L2_gnn_setup()
    _L2_gnn_in = {k: v for k, v in _L2_gnn_all.items() if k in ('Wl', 'bl', 'Ws', 'bs', 'Wr', 'br', 'ln_w', 'ln_b')}
    del _L2_gnn_all

    def _L3_gnn_setup():
        import jax, jax.numpy as jnp
        import numpy as np
        NUM_HEADS = 12
        HIDDEN = 384
        HEAD = HIDDEN // NUM_HEADS
        SCALE = HIDDEN ** (-0.5)
        key = jax.random.key(seed)
        ks = jax.random.split(key, 8)
        B, N = (16, 256)
        std = HIDDEN ** (-0.5)
        return {'x': jax.random.normal(ks[0], (B, N, HIDDEN), dtype=jnp.float32), 'encoding_bias': jax.random.normal(ks[1], (B, N, N), dtype=jnp.float32), 'Wq': jax.random.normal(ks[2], (HIDDEN, HIDDEN), dtype=jnp.float32) * std, 'Wk': jax.random.normal(ks[3], (HIDDEN, HIDDEN), dtype=jnp.float32) * std, 'Wv': jax.random.normal(ks[4], (HIDDEN, HIDDEN), dtype=jnp.float32) * std, 'bv': jax.random.normal(ks[5], (HIDDEN,), dtype=jnp.float32) * 0.01, 'Wo': jax.random.normal(ks[6], (HIDDEN, HIDDEN), dtype=jnp.float32) * std, 'bo': jax.random.normal(ks[7], (HIDDEN,), dtype=jnp.float32) * 0.01}
    _L3_gnn_all = _L3_gnn_setup()
    _L3_gnn_in = {k: v for k, v in _L3_gnn_all.items() if k in ('Wq', 'Wk', 'Wv', 'bv', 'Wo', 'bo')}
    del _L3_gnn_all
    return {'x': x, 'adj': adj, 'L0_gnn_Wq': _L0_gnn_in['Wq'], 'L0_gnn_Wk': _L0_gnn_in['Wk'], 'L0_gnn_Wv': _L0_gnn_in['Wv'], 'L0_gnn_bv': _L0_gnn_in['bv'], 'L0_gnn_Wo': _L0_gnn_in['Wo'], 'L0_gnn_bo': _L0_gnn_in['bo'], 'L1_gnn_Wq': _L1_gnn_in['Wq'], 'L1_gnn_bq': _L1_gnn_in['bq'], 'L1_gnn_Wk': _L1_gnn_in['Wk'], 'L1_gnn_bk': _L1_gnn_in['bk'], 'L1_gnn_Wv': _L1_gnn_in['Wv'], 'L1_gnn_bv': _L1_gnn_in['bv'], 'L1_gnn_beta': _L1_gnn_in['beta'], 'L2_gnn_Wl': _L2_gnn_in['Wl'], 'L2_gnn_bl': _L2_gnn_in['bl'], 'L2_gnn_Ws': _L2_gnn_in['Ws'], 'L2_gnn_bs': _L2_gnn_in['bs'], 'L2_gnn_Wr': _L2_gnn_in['Wr'], 'L2_gnn_br': _L2_gnn_in['br'], 'L2_gnn_ln_w': _L2_gnn_in['ln_w'], 'L2_gnn_ln_b': _L2_gnn_in['ln_b'], 'L3_gnn_Wq': _L3_gnn_in['Wq'], 'L3_gnn_Wk': _L3_gnn_in['Wk'], 'L3_gnn_Wv': _L3_gnn_in['Wv'], 'L3_gnn_bv': _L3_gnn_in['bv'], 'L3_gnn_Wo': _L3_gnn_in['Wo'], 'L3_gnn_bo': _L3_gnn_in['bo']}

def reference(x, adj, L0_gnn_Wq, L0_gnn_Wk, L0_gnn_Wv, L0_gnn_bv, L0_gnn_Wo, L0_gnn_bo, L1_gnn_Wq, L1_gnn_bq, L1_gnn_Wk, L1_gnn_bk, L1_gnn_Wv, L1_gnn_bv, L1_gnn_beta, L2_gnn_Wl, L2_gnn_bl, L2_gnn_Ws, L2_gnn_bs, L2_gnn_Wr, L2_gnn_br, L2_gnn_ln_w, L2_gnn_ln_b, L3_gnn_Wq, L3_gnn_Wk, L3_gnn_Wv, L3_gnn_bv, L3_gnn_Wo, L3_gnn_bo):
    import jax
    import jax.numpy as jnp

    def _L0_gnn_ref(x, spatial_encoding, edge_encoding, Wq, Wk, Wv, bv, Wo, bo):
        import jax, jax.numpy as jnp
        import numpy as np
        NUM_HEADS = 12
        HIDDEN = 384
        HEAD = HIDDEN // NUM_HEADS
        B, N = (16, 256)
        b, n, h = x.shape
        scale = jnp.asarray(HIDDEN, x.dtype) ** (-0.5)
        q = (x @ Wq.T).reshape(b, n, NUM_HEADS, HEAD)
        k = (x @ Wk.T).reshape(b, n, NUM_HEADS, HEAD)
        v = (x @ Wv.T + bv).reshape(b, n, NUM_HEADS, HEAD)
        bias = (spatial_encoding + edge_encoding)[:, None]
        scores = jnp.einsum('bqhd,bkhd->bhqk', q, k) * scale + bias
        row_nonzero = jnp.any(scores != 0, axis=-1, keepdims=True)
        scores = jnp.where(row_nonzero, scores, -jnp.inf)
        p = jax.nn.softmax(scores, axis=-1)
        p = jnp.nan_to_num(p)
        out = jnp.einsum('bhqk,bkhd->bqhd', p, v).reshape(b, n, h)
        return out @ Wo.T + bo

    def _L1_gnn_ref(input_graph, adj, Wq, bq, Wk, bk, Wv, bv, beta):
        import jax, jax.numpy as jnp
        import numpy as np
        B, N, D, H = (8, 512, 384, 12)
        HD = D // H

        def _split_heads(x):
            b, n, _ = x.shape
            return x.reshape(b, n, H, HD).transpose(0, 2, 1, 3)
        q = _split_heads(input_graph @ Wq + bq)
        k = _split_heads(input_graph @ Wk + bk)
        v = _split_heads(input_graph @ Wv + bv)
        scores = jnp.einsum('bhqd,bhkd->bhqk', q, k) / jnp.sqrt(jnp.asarray(HD, input_graph.dtype))
        adj_e = adj[:, None, :, :]
        scores = scores + beta * adj_e
        scores = jnp.where(adj_e > 0, scores, jnp.asarray(-9000000000000000.0, scores.dtype))
        probs = jax.nn.softmax(scores, axis=-1)
        out = jnp.einsum('bhqk,bhkd->bhqd', probs, v)
        return out.transpose(0, 2, 1, 3).reshape(input_graph.shape[0], input_graph.shape[1], D)

    def _L2_gnn_ref(hidden_state, adjacency_matrix, Wl, bl, Ws, bs, Wr, br, ln_w, ln_b):
        import jax, jax.numpy as jnp
        import numpy as np
        LN_EPS = 1e-12

        def _digcn_forward(hidden_state, adjacency_matrix, Wl, bl, Ws, bs, Wr, br, ln_w, ln_b):
            B, S, D = hidden_state.shape
            temper = jnp.asarray(D, jnp.float32) ** 0.5
            i = jnp.arange(S)
            upper = (i[None, :] > i[:, None]).astype(hidden_state.dtype)
            lower = (i[None, :] < i[:, None]).astype(hidden_state.dtype)

            def layer(h, params):
                wl, b_l, ws, b_s, wr, b_r, g, beta = params
                u = jnp.einsum('bid,bjd->bij', h, h) / temper
                a = jax.nn.softmax(u, axis=-1)
                delta = a * adjacency_matrix
                attn = delta / (jnp.sum(delta, axis=-1, keepdims=True) + 1e-10)
                hl = h @ wl.T + b_l
                hs = h @ ws.T + b_s
                hr = h @ wr.T + b_r
                diag_a = jnp.diagonal(attn, axis1=1, axis2=2)
                ctx = jnp.einsum('bij,bjd->bid', attn * upper, hl) + diag_a[..., None] * hs + jnp.einsum('bij,bjd->bid', attn * lower, hr)
                mean = ctx.mean(-1, keepdims=True)
                var = ctx.var(-1, keepdims=True)
                o = (ctx - mean) / jnp.sqrt(var + LN_EPS) * g + beta
                return (jax.nn.relu(o), None)
            out, _ = jax.lax.scan(layer, hidden_state, (Wl, bl, Ws, bs, Wr, br, ln_w, ln_b))
            return out
        return _digcn_forward(hidden_state, adjacency_matrix, Wl, bl, Ws, bs, Wr, br, ln_w, ln_b)

    def _L3_gnn_ref(x, encoding_bias, Wq, Wk, Wv, bv, Wo, bo):
        import jax, jax.numpy as jnp
        import numpy as np
        NUM_HEADS = 12
        HIDDEN = 384
        HEAD = HIDDEN // NUM_HEADS
        SCALE = HIDDEN ** (-0.5)
        B, N, _ = x.shape
        q = (x @ Wq.T).reshape(B, N, NUM_HEADS, HEAD)
        k = (x @ Wk.T).reshape(B, N, NUM_HEADS, HEAD)
        v = (x @ Wv.T + bv).reshape(B, N, NUM_HEADS, HEAD)
        a = jnp.einsum('bnhd,bmhd->bhnm', q, k) * SCALE + encoding_bias[:, None, :, :]
        pad_mask = jnp.all(a == 0, axis=-1)
        a = jnp.where(pad_mask[..., None], -jnp.inf, a)
        a = jax.nn.softmax(a, axis=-1)
        a = jnp.nan_to_num(a)
        o = jnp.einsum('bhnm,bmhd->bnhd', a, v).reshape(B, N, HIDDEN)
        return o @ Wo.T + bo
    x = _layernorm(x + _L0_gnn_ref(x, adj, adj, L0_gnn_Wq, L0_gnn_Wk, L0_gnn_Wv, L0_gnn_bv, L0_gnn_Wo, L0_gnn_bo), axis=-1)
    x = _layernorm(x + _L1_gnn_ref(x, adj, L1_gnn_Wq, L1_gnn_bq, L1_gnn_Wk, L1_gnn_bk, L1_gnn_Wv, L1_gnn_bv, L1_gnn_beta), axis=-1)
    x = _layernorm(x + _L2_gnn_ref(x, adj, L2_gnn_Wl, L2_gnn_bl, L2_gnn_Ws, L2_gnn_bs, L2_gnn_Wr, L2_gnn_br, L2_gnn_ln_w, L2_gnn_ln_b), axis=-1)
    x = _layernorm(x + _L3_gnn_ref(x, adj, L3_gnn_Wq, L3_gnn_Wk, L3_gnn_Wv, L3_gnn_bv, L3_gnn_Wo, L3_gnn_bo), axis=-1)
    return x

_drawn_inputs = setup_inputs


def setup_inputs(seed=0):
    import zlib

    import numpy as np

    out = dict(_drawn_inputs(seed))
    spreads = {'L1_gnn_bq': (0.0, 0.1),
     'L1_gnn_bk': (0.0, 2.0),
     'L1_gnn_bv': (0.0, 0.1),
     'L2_gnn_bl': (0.0, 2.0),
     'L2_gnn_bs': (0.0, 0.1),
     'L2_gnn_br': (0.0, 2.0),
     'L2_gnn_ln_w': (1.0, 0.2),
     'L2_gnn_ln_b': (0.0, 0.1)}
    factors = {'L0_gnn_Wq': 8.0,
     'L0_gnn_Wk': 8.0,
     'L0_gnn_bv': 3.827,
     'L2_gnn_Wl': 3.394,
     'L2_gnn_Wr': 4.28,
     'L3_gnn_bv': 5.63,
     'L3_gnn_bo': 6.213}
    for name, (base, spread) in spreads.items():
        noise = np.random.default_rng([zlib.crc32(name.encode()), seed]).standard_normal(out[name].shape)
        drawn = base * np.exp(spread * noise) if base else spread * noise
        out[name] = jnp.asarray(drawn.astype(out[name].dtype))
    for name, factor in factors.items():
        out[name] = (out[name] * factor).astype(out[name].dtype)
    return out
```

```python
from contextlib import ExitStack

import concourse.bass as bass
from concourse import mybir

F32 = mybir.dt.float32
F32R = mybir.dt.float32r
ALU = mybir.AluOpType
ACT = mybir.ActivationFunctionType
AX = mybir.AxisListType

P = 128
NODES = 64
D = 384
KT = D // P
HEADS = 12
PAIRS = HEADS // 2
GPU = P // NODES
UNITS = 4
ROWS = P * UNITS
LN_EPS = 1e-5
LN_EPS_INNER = 1e-12
MASKED = -9000000000000000.0
SPLIT = ((0, 0), (1, 0), (0, 1))


def counted(value):
    return not isinstance(value, int) or value > 0


def inside(index, count):
    return not isinstance(index, int) or 0 <= index < count


def over_groups(eng, groups, group, peel_first=True):
    pairs = groups // 2
    for par in range(2):
        group(par, 0, par)
    with eng.Fori(1, pairs - 1) as pair:
        for par in range(2):
            group(pair * 2 + par, pair, par)
    for par in range(2):
        group(groups - 2 + par, pairs - 1, par)


class Pass:

    def __init__(self, nc, ctx, tag):
        self.nc, self.ctx, self.tag, self.sems = nc, ctx, tag, []

    def sb(self, name, shape, dt=F32):
        return self.ctx.enter_context(self.nc.sbuf_tensor(f"{self.tag}_{name}", shape, dt))

    def ps(self, name, shape):
        return self.ctx.enter_context(self.nc.psum_tensor(f"{self.tag}_{name}", shape, F32))

    def sem(self, name):
        self.sems.append(self.nc.alloc_semaphore(f"{self.tag}_{name}"))
        return self.sems[-1]


def attention_pass(nc, tag, src, dst, adj, weights, scale, transposed, wo, bv, bo, beta, edge_factor, groups):
    units = groups * UNITS
    mats, row_bias_cols = weights
    NM = len(mats)
    src_g = src.rearrange("(i u p) d -> i p u d", u=UNITS, p=P)
    adj_g = adj.rearrange("(i u p) k -> i p u k", u=UNITS, p=P)
    src_u = src.rearrange("(i u p) d -> i u p d", u=UNITS, p=P)
    dst_u = dst.rearrange("(i u p) d -> i u p d", u=UNITS, p=P)

    with ExitStack() as ctx:
        a = Pass(nc, ctx, tag)
        W = [a.sb(f"w{m}", [P, 2, KT, D], F32R) for m in range(NM)]
        raw = [a.sb(f"raw{m}", [P, KT, D]) for m in range(2)]
        ident = a.sb("ident", [P, P])
        ones = a.sb("ones", [P, P])
        pick = a.sb("pick", [P, P], F32R)
        brow = a.sb("brow", [P, 2, D])
        bround = a.sb("bround", [P, 2, D], F32R)
        bias = a.sb("bias", [P, 2, D], F32R)
        qkb = a.sb("qkb", [P, 2, KT])
        betas = a.sb("betas", [P, 1])
        mhalf = a.sb("mhalf", [P, 1])
        epst = a.sb("epst", [P, 1])
        xa = a.sb("xa", [P, UNITS, D])
        xT = a.sb("xT", [P, 2, KT, ROWS], F32R)
        edge = [a.sb(f"edge{b}", [P, UNITS, NODES]) for b in range(2)]
        off = a.sb("off", [P, UNITS, NODES])
        sbias = [a.sb(f"sbias{b}", [P, UNITS, NODES]) for b in range(2)]
        qT = [a.sb(f"qT{b}", [P, KT, ROWS]) for b in range(2)]
        kT = [a.sb(f"kT{b}", [P, KT, ROWS]) for b in range(2)]
        v2 = [a.sb(f"v2{b}", [P, UNITS * GPU, PAIRS, 64]) for b in range(2)]
        k4 = [a.sb(f"k4{b}", [P, GPU, KT, 4, NODES]) for b in range(2)]
        sc = [a.sb(f"sc{b}", [P, HEADS, NODES]) for b in range(2)]
        pr = [a.sb(f"pr{b}", [P, HEADS, NODES]) for b in range(2)]
        st = [a.sb(f"st{b}", [P, 6, HEADS]) for b in range(2)]
        pT = [a.sb(f"pT{b}", [P, PAIRS, P]) for b in range(2)]
        oT = [a.sb(f"oT{b}", [P, 2, KT, P], F32R if wo else F32) for b in range(2)]
        xr = [a.sb(f"xr{b}", [P, D]) for b in range(2)]
        res = [a.sb(f"res{b}", [P, D]) for b in range(2)]
        ln = [a.sb(f"ln{b}", [P, 10]) for b in range(2)]
        yo = [a.sb(f"yo{b}", [P, D]) for b in range(2)]

        ps_s = a.ps("ps_s", [P, 2 * 512])
        ps_t = a.ps("ps_t", [P, 2 * 512])
        ps_o = a.ps("ps_o", [P, 512])
        ps_y = a.ps("ps_y", [P, 512])
        ps_p = [a.ps(f"ps_p{b}", [P, 512]) for b in range(2)]

        s_raw = [a.sem(f"s_raw{b}") for b in range(2)]
        s_small = a.sem("s_small")
        c_ident, c_zero, c_one, c_row = (a.sem(x) for x in ("c_ident", "c_zero", "c_one", "c_row"))
        pe_w, act_w, dve_w = a.sem("pe_w"), a.sem("act_w"), a.sem("dve_w")
        s_xa = a.sem("s_xa")
        s_edge = [a.sem(f"s_edge{b}") for b in range(2)]
        s_xr = [a.sem(f"s_xr{b}") for b in range(2)]
        s_out = [a.sem(f"s_out{b}") for b in range(2)]
        pe_x, pe_p, pe_s, pe_t, pe_o, pe_y = (a.sem(x) for x in ("pe_x", "pe_p", "pe_s", "pe_t", "pe_o", "pe_y"))
        act_x, act_qk, act_v, act_e, act_pT, act_o = (
            a.sem(x) for x in ("act_x", "act_qk", "act_v", "act_e", "act_pT", "act_o"))
        dve_x, dve_off, dve_bias, dve_k4, dve_sc, dve_mx, dve_mn, dve_sum, dve_inv, dve_o = (
            a.sem(x) for x in ("dve_x", "dve_off", "dve_bias", "dve_k4", "dve_sc", "dve_mx", "dve_mn",
                               "dve_sum", "dve_inv", "dve_o"))
        dve_m0, dve_rinv, dve_res, dve_bn, dve_mv, dve_y = (
            a.sem(x) for x in ("dve_m0", "dve_rinv", "dve_res", "dve_bn", "dve_mv", "dve_y"))
        pool_sub, pool_p, pool_ve, pool_rs = (a.sem(x) for x in ("pool_sub", "pool_p", "pool_ve", "pool_rs"))

        n_small = sum(x is not None for x in (bv, bo)) * 2 + (2 if row_bias_cols else 0) + (beta is not None)
        steps = NM * KT
        zeros = 2 + 2 + 1 + 1

        block = ctx.enter_context(nc.Block())

        @block.sync
        def _(sp):
            for m in range(NM):
                if m >= 2:
                    if counted(KT * (m - 1)):
                        sp.wait_ge(dve_w, KT * (m - 1))
                sp.dma_start(raw[m % 2][:, :, :], mats[m].rearrange("(t p) n -> p t n", p=P)).then_inc(s_raw[m % 2], 16)
                if m == 1:
                    sp.dma_start(xa[:, :, :], src_g[0]).then_inc(s_xa, 16)
                    sp.dma_start(edge[0][:, :, :], adj_g[0]).then_inc(s_edge[0], 16)
                    for j, b in enumerate((bv, bo)):
                        if b is not None:
                            for row in (0, 32):
                                sp.dma_start(brow[row:row + 1, j, :], b.rearrange("(a d) -> a d", a=1)).then_inc(s_small, 16)
                    for j, b in enumerate(row_bias_cols or ()):
                        sp.dma_start(qkb[:, j, :], b.rearrange("(t p) -> p t", p=P),
                                     allow_slow_non_contiguous=True).then_inc(s_small, 16)
                    if beta is not None:
                        sp.dma_start(betas[:, :], beta.to_broadcast([P, 1])).then_inc(s_small, 16)
            sp.wait_ge(pe_x, KT)
            sp.dma_start(xa[:, :, :], src_g[1]).then_inc(s_xa, 16)

            def store(n, i, s, half):
                if inside(n, units):
                    sp.wait_ge(dve_y, n + 1)
                    sp.dma_start(dst_u[i, s], yo[s % 2][:, :]).then_inc(s_out[s % 2], 16)

            def group(i, pair, par):
                for s in range(UNITS):
                    n = i * UNITS + s
                    if s == 0 and inside(i + 1, groups):
                        if counted((i - 1) * UNITS + UNITS):
                            sp.wait_ge(dve_sc, (i - 1) * UNITS + UNITS)
                        sp.dma_start(edge[1 - par][:, :, :], adj_g[i + 1]).then_inc(s_edge[1 - par], 16)
                    if s == 0 and inside(i + 2, groups):
                        sp.wait_ge(pe_x, KT * (i + 2))
                        sp.dma_start(xa[:, :, :], src_g[i + 2]).then_inc(s_xa, 16)
                    if counted(n - 1):
                        sp.wait_ge(dve_res, n - 1)
                    sp.dma_start(xr[s % 2][:, :], src_u[i, s]).then_inc(s_xr[s % 2], 16)
                    if s >= 2:
                        store(n - 2, i, s - 2, None)
                    else:
                        store(n - 2, i - 1, s + 2, None)

            over_groups(sp, groups, group)
            store(units - 2, groups - 1, 2, None)
            store(units - 1, groups - 1, 3, None)
            for b in range(2):
                sp.wait_ge(s_out[b], 16 * (units // 2))

        @block.gpsimd
        def _(pool):
            nc.gpsimd.memset(ones[:, :], 1.0).then_inc(c_one, 1)
            nc.gpsimd.memset(mhalf[:, :], -0.5).then_inc(c_one, 1)
            nc.gpsimd.memset(epst[:, :], LN_EPS).then_inc(c_one, 1)
            pool.wait_ge(c_one, 3)
            nc.gpsimd.affine_select(out=ident[:, :], in_=ones[:, :], compare_op=ALU.is_equal, fill=0.0,
                                    base=0, pattern=[[-1, P]], channel_multiplier=1).then_inc(c_ident, 1)

            def rstd(n, b):
                if inside(n, units):
                    pool.wait_ge(dve_mv, n + 1)
                    nc.gpsimd.tensor_tensor(ln[b][:, 8:9], ln[b][:, 7:8], epst[:, :], ALU.add).then_inc(pool_ve, 1)
                    pool.wait_ge(pool_ve, n + 1)
                    nc.gpsimd.tensor_tensor(ln[b][:, 9:10], ln[b][:, 8:9], mhalf[:, :], ALU.pow).then_inc(pool_rs, 1)

            def group(i, pair, par):
                for s in range(UNITS):
                    n, b = i * UNITS + s, s % 2
                    rstd(n - 2, b)
                    pool.wait_ge(dve_mx, n + 1)
                    if counted(2 * (n - 1)):
                        pool.wait_ge(pe_t, 2 * (n - 1))
                    nc.gpsimd.tensor_tensor(pr[b][:, :, :], sc[b][:, :, :],
                                            st[b][:, 0, :].unsqueeze(2).to_broadcast([P, HEADS, NODES]),
                                            ALU.subtract).then_inc(pool_sub, 1)
                    pool.wait_ge(dve_rinv, n + 1)
                    nc.gpsimd.tensor_tensor(pr[b][:, :, :], pr[b][:, :, :],
                                            st[b][:, 5, :].unsqueeze(2).to_broadcast([P, HEADS, NODES]),
                                            ALU.mult).then_inc(pool_p, 1)

            over_groups(pool, groups, group)
            rstd(units - 2, 0)
            rstd(units - 1, 1)

        @block.tensor
        def _(pe):
            pe.wait_ge(c_ident, 1)
            if transposed:
                for m in range(NM):
                    pe.wait_ge(s_raw[m % 2], 16 * (m // 2 + 1))
                    for t in range(KT):
                        step = m * KT + t
                        if counted(step - 1):
                            pe.wait_ge(dve_w, step - 1)
                        for o in range(KT):
                            last = nc.tensor.transpose(ps_p[step % 2][:, o * P:(o + 1) * P],
                                                       raw[m % 2][:, o, t * P:(t + 1) * P], ident[:, :])
                        last.then_inc(pe_w, 1)

            def bank_free(g, idx):
                if idx < 2:
                    pe.wait_ge(dve_x, KT * g + idx + 2)
                elif idx < 8:
                    if counted(6 * g + idx - 1):
                        pe.wait_ge(act_qk, 6 * g + idx - 1)
                elif idx < 12:
                    if counted(UNITS * g + idx - 7):
                        pe.wait_ge(act_v, UNITS * g + idx - 7)
                else:
                    pe.wait_ge(dve_x, KT * (g + 1) + 1)

            def rows_T(g, gpar):
                if not inside(g, groups):
                    return
                pe.wait_ge(s_xa, 16 * (g + 1))
                for t in range(KT):
                    if isinstance(g, int) and g == 0:
                        pe.wait_ge(dve_w, steps)
                        if counted(t - 1):
                            pe.wait_ge(dve_x, t - 1)
                    else:
                        bank_free(g - 1, 10 + t)
                    bank = ps_p[(t + gpar + 1) % 2]
                    for u in range(UNITS):
                        last = nc.tensor.transpose(bank[:, u * P:(u + 1) * P], xa[:, u, t * P:(t + 1) * P], ident[:, :])
                    last.then_inc(pe_x, 1)

            def project(g, gpar, idx):
                if not inside(g, groups):
                    return
                bank = ps_p[(gpar + idx) % 2]
                bank_free(g, idx)
                pe.wait_ge(act_x, KT * (g + 1))
                pe.wait_ge(dve_x, KT * (g + 1))
                if idx < 6:
                    m, o = divmod(idx, 3)
                    for c, (l, r) in enumerate(SPLIT):
                        for t in range(KT):
                            last = nc.tensor.matmul(bank[:, :], W[m][:, l, t, o * P:(o + 1) * P], xT[:, r, t, :],
                                                    start=c + t == 0, stop=c == 2 and t == KT - 1)
                else:
                    u = idx - 6
                    for c, (l, r) in enumerate(SPLIT):
                        for t in range(KT):
                            last = nc.tensor.matmul(bank[:, :D], xT[:, l, t, u * P:(u + 1) * P], W[2][:, r, t, :],
                                                    start=c + t == 0, stop=False)
                    last = nc.tensor.matmul(bank[:, :D], pick[:, :], bias[:, 0, :], start=False, stop=True)
                last.then_inc(pe_p, 1)

            def scores(n, par, s):
                if not inside(n, units):
                    return
                pe.wait_ge(dve_k4, n + 1)
                if counted(n):
                    pe.wait_ge(dve_sc, n)
                for t in range(KT):
                    for g in range(GPU):
                        c = s * P + g * NODES
                        last = nc.tensor.matmul(ps_s[g * NODES:(g + 1) * NODES, t * 256:(t + 1) * 256],
                                                qT[par][:, t, c:c + NODES], k4[s % 2][:, g, t, :, :],
                                                start=True, stop=True)
                last.then_inc(pe_s, 1)

            def probs_T(n, b):
                if not inside(n, units):
                    return
                pe.wait_ge(pool_p, n + 1)
                for h in range(PAIRS):
                    if h in (0, 4):
                        if counted(2 * n - 1 + (h == 4)):
                            pe.wait_ge(act_pT, 2 * n - 1 + (h == 4))
                    last = nc.tensor.transpose(ps_t[:, h * P:(h + 1) * P], pr[b][:, 2 * h:2 * h + 2, :], ident[:, :])
                    if h in (3, 5):
                        last.then_inc(pe_t, 1)

            def values(n, par, s):
                if not inside(n, units):
                    return
                pe.wait_ge(act_pT, 2 * (n + 1))
                pe.wait_ge(act_v, n + 1)
                if counted(n):
                    pe.wait_ge(act_o, n)
                if wo:
                    if counted(n):
                        pe.wait_ge(dve_o, n)
                for h in range(PAIRS):
                    for g in range(GPU):
                        r = 64 * (h % 2)
                        last = nc.tensor.matmul(ps_o[r:r + 64, (h // 2) * P + g * NODES:(h // 2) * P + (g + 1) * NODES],
                                                v2[par][:, GPU * s + g, h, :], pT[s % 2][:, h, g * NODES:(g + 1) * NODES],
                                                start=True, stop=True)
                last.then_inc(pe_o, 1)

            def output(n, b):
                if not inside(n, units):
                    return
                pe.wait_ge(act_o, n + 1)
                if counted(n):
                    pe.wait_ge(dve_res, n)
                if wo:
                    pe.wait_ge(dve_o, n + 1)
                    for c, (l, r) in enumerate(SPLIT):
                        for t in range(KT):
                            nc.tensor.matmul(ps_y[:, :D], oT[b][:, l, t, :], W[3][:, r, t, :], start=c + t == 0, stop=False)
                    last = nc.tensor.matmul(ps_y[:, :D], pick[:, :], bias[:, 1, :], start=False, stop=True)
                else:
                    for t in range(KT):
                        last = nc.tensor.transpose(ps_y[:, t * P:(t + 1) * P], oT[b][:, 0, t, :], ident[:, :])
                last.then_inc(pe_y, 1)

            rows_T(0, 0)
            pe.wait_ge(act_w, steps)
            pe.wait_ge(dve_w, steps)
            pe.wait_ge(c_row, 2 * sum(x is not None for x in (bv, bo)) + 2)
            for idx in range(10):
                project(0, 0, idx)
            rows_T(1, 1)
            pe.wait_ge(c_zero, zeros)

            between = {0: ((), (0,), (1,)), 1: ((2,), (3,), (4,)), 2: ((5,), (6,), (7,)), 3: ((8,), (9,), ("x",))}

            def fill(i, par, s, c):
                for item in between[s][c]:
                    if item == "x":
                        rows_T(i + 2, par)
                    else:
                        project(i + 1, 1 - par, item)

            def group(i, pair, par):
                for s in range(UNITS):
                    n = i * UNITS + s
                    ppar, ps = (par, s - 1) if s else (1 - par, UNITS - 1)
                    scores(n, par, s)
                    fill(i, par, s, 0)
                    probs_T(n - 1, ps % 2)
                    fill(i, par, s, 1)
                    values(n - 1, ppar, ps)
                    fill(i, par, s, 2)
                    output(n - 1, ps % 2)

            over_groups(pe, groups, group)
            probs_T(units - 1, 1)
            values(units - 1, 1, UNITS - 1)
            output(units - 1, 1)

        @block.scalar
        def _(act):
            for step in range(steps):
                m, t = divmod(step, KT)
                if transposed:
                    act.wait_ge(pe_w, step + 1)
                    nc.scalar.activation(W[m][:, 0, t, :], ps_p[step % 2][:, :D], ACT.Copy).then_inc(act_w, 1)
                else:
                    act.wait_ge(s_raw[m % 2], 16 * (m // 2 + 1))
                    nc.scalar.activation(W[m][:, 0, t, :], raw[m % 2][:, t, :], ACT.Copy).then_inc(act_w, 1)
            act.wait_ge(s_small, 16 * n_small)
            act.wait_ge(c_zero, zeros)
            for j, b in enumerate((bv, bo)):
                if b is not None:
                    nc.scalar.activation(bias[0:1, j, :], brow[0:1, j, :], ACT.Copy).then_inc(c_row, 1)
                    nc.scalar.activation(bround[32:33, j, :], brow[32:33, j, :], ACT.Copy).then_inc(act_w, 1)

            def rows_T(g):
                if not inside(g, groups):
                    return
                for t in range(KT):
                    act.wait_ge(pe_x, KT * g + t + 1)
                    nc.scalar.activation(xT[:, 0, t, :], ps_p[pbank(g, t)][:, :], ACT.Copy).then_inc(act_x, 1)

            def taken(g, gpar, idx):
                if not inside(g, groups):
                    return
                bank = ps_p[(gpar + idx) % 2]
                act.wait_ge(pe_p, 10 * g + idx + 1)
                if idx < 6:
                    m, o = divmod(idx, 3)
                    if not inside(g - 2, groups):
                        pass
                    else:
                        if counted(UNITS * (g - 1)):
                            act.wait_ge(pe_s, UNITS * (g - 1))
                        if counted(UNITS * (g - 1)):
                            act.wait_ge(dve_k4, UNITS * (g - 1))
                    out = (qT, kT)[m][gpar][:, o, :]
                    if row_bias_cols:
                        i = nc.scalar.activation(out, bank[:, :], ACT.Identity, bias=qkb[:, m, o:o + 1])
                    else:
                        i = nc.scalar.activation(out, bank[:, :], ACT.Copy)
                    i.then_inc(act_qk, 1)
                else:
                    u = idx - 6
                    if counted(UNITS * (g - 2) + u + 1):
                        act.wait_ge(pe_o, UNITS * (g - 2) + u + 1)
                    for g2 in range(GPU):
                        for odd in range(2):
                            got = bank[g2 * NODES:(g2 + 1) * NODES, :D].rearrange("p (h o d) -> p h o d", o=2, d=32)
                            i = nc.scalar.activation(v2[gpar][64 * odd:64 * odd + 64, GPU * u + g2, :, 32 * odd:32 * odd + 32],
                                                     got[:, :, odd, :], ACT.Copy)
                    i.then_inc(act_v, 1)

            def pbank(g, t):
                return (t + gp[0] + 1) % 2

            gp = [0]
            rows_T(0)
            for idx in range(10):
                taken(0, 0, idx)
            gp[0] = 1
            rows_T(1)

            between = {0: ((), (0,), (1,)), 1: ((2,), (3,), (4,)), 2: ((5,), (6,), (7,)), 3: ((8,), (9,), ("x",))}

            def fill(i, par, s, c):
                for item in between[s][c]:
                    if item == "x":
                        gp[0] = par
                        rows_T(i + 2)
                    else:
                        taken(i + 1, 1 - par, item)

            def probs_T(n, b):
                if not inside(n, units):
                    return
                for half, (lo, hi) in enumerate(((0, 4), (4, 6))):
                    act.wait_ge(pe_t, 2 * n + half + 1)
                    if counted(n - 1):
                        act.wait_ge(pe_o, n - 1)
                    nc.scalar.activation(pT[b][:, lo:hi, :], ps_t[:, lo * P:hi * P].rearrange("p (h q) -> p h q", q=P),
                                         ACT.Copy).then_inc(act_pT, 1)

            def values(n, b):
                if not inside(n, units):
                    return
                act.wait_ge(pe_o, n + 1)
                if counted(n - 1):
                    act.wait_ge(pe_y, n - 1)
                if wo:
                    if counted(n - 1):
                        act.wait_ge(dve_o, n - 1)
                nc.scalar.activation(oT[b][:, 0, :, :], ps_o[:, :D].rearrange("p (t q) -> p t q", q=P),
                                     ACT.Copy).then_inc(act_o, 1)

            def group(i, pair, par):
                for s in range(UNITS):
                    n = i * UNITS + s
                    fill(i, par, s, 0)
                    probs_T(n - 1, (s - 1) % 2)
                    act.wait_ge(pool_sub, n + 1)
                    nc.scalar.activation(pr[s % 2][:, :, :], pr[s % 2][:, :, :], ACT.Exp).then_inc(act_e, 1)
                    fill(i, par, s, 1)
                    values(n - 1, (s - 1) % 2)
                    fill(i, par, s, 2)

            over_groups(act, groups, group)
            probs_T(units - 1, 1)
            values(units - 1, 1)

        @block.vector
        def _(dve):
            nc.vector.memset(pick[:, :].bitcast(F32), 0.0).then_inc(c_zero, 1)
            nc.vector.memset(bias[:, :, :].bitcast(F32), 0.0).then_inc(c_zero, 1)
            for b in range(2):
                nc.vector.memset(v2[b][:, :, :, :], 0.0).then_inc(c_zero, 1)
                nc.vector.memset(k4[b][:, :, :, :, :], 0.0).then_inc(c_zero, 1)
            dve.wait_ge(c_one, 1)
            dve.wait_ge(c_zero, zeros)
            for row in (0, 32):
                nc.vector.tensor_copy(pick[row:row + 1, :], ones[row:row + 1, :]).then_inc(c_row, 1)
            for step in range(steps):
                m, t = divmod(step, KT)
                dve.wait_ge(act_w, step + 1)
                got = ps_p[step % 2][:, :D] if transposed else raw[m % 2][:, t, :]
                nc.vector.tensor_tensor(W[m][:, 1, t, :], got, W[m][:, 0, t, :].bitcast(F32),
                                        ALU.subtract).then_inc(dve_w, 1)
            rows = [j for j, b in enumerate((bv, bo)) if b is not None]
            if counted(steps + len(rows)):
                dve.wait_ge(act_w, steps + len(rows))
            for j in rows:
                nc.vector.tensor_tensor(bias[32:33, j, :], brow[32:33, j, :], bround[32:33, j, :].bitcast(F32),
                                        ALU.subtract).then_inc(c_row, 1)

            def rows_T(g, gpar):
                if not inside(g, groups):
                    return
                for t in range(KT):
                    dve.wait_ge(act_x, KT * g + t + 1)
                    nc.vector.tensor_tensor(xT[:, 1, t, :], ps_p[(t + gpar + 1) % 2][:, :],
                                            xT[:, 0, t, :].bitcast(F32), ALU.subtract).then_inc(dve_x, 1)

            def edges(g, pair, gpar):
                if not inside(g, groups):
                    return
                dve.wait_ge(s_edge[gpar], 16 * (pair + 1))
                if beta is not None:
                    dve.wait_ge(dve_bias, g)
                    nc.vector.tensor_scalar(off[:, :, :], edge[gpar][:, :, :], 0.0, MASKED, ALU.is_le, ALU.mult).then_inc(dve_off, 1)
                    dve.wait_ge(dve_off, g + 1)
                    nc.vector.scalar_tensor_tensor(out=sbias[gpar][:, :, :], in0=edge[gpar][:, :, :], scalar=betas[:, 0:1],
                                                   in1=off[:, :, :], op0=ALU.mult, op1=ALU.add).then_inc(dve_bias, 1)
                else:
                    nc.vector.tensor_scalar(sbias[gpar][:, :, :], edge[gpar][:, :, :], edge_factor, 0.0, ALU.mult, ALU.add).then_inc(dve_bias, 1)

            def spread(n, i, par, s):
                if not inside(n, units):
                    return
                dve.wait_ge(act_qk, 6 * (i + 1))
                if counted(n - 1):
                    dve.wait_ge(pe_s, n - 1)
                for j in range(4):
                    q = slice(32 * j, 32 * j + 32)
                    got = kT[par][q, :, s * P:(s + 1) * P].rearrange("p t (g k) -> p g t k", g=GPU)
                    for g in range(GPU):
                        last = nc.vector.tensor_copy(k4[s % 2][q, g, :, j, :], got[:, g, :, :])
                last.then_inc(dve_k4, 1)

            def softmax_max(n, par, s):
                b = s % 2
                dve.wait_ge(pe_s, n + 1)
                dve.wait_ge(dve_bias, ni[0] + 1)
                if counted(n - 1):
                    dve.wait_ge(pool_sub, n - 1)
                nc.vector.scalar_tensor_tensor(
                    out=sc[b][:, :, :], in0=ps_s[:, :HEADS * NODES].rearrange("p (h k) -> p h k", k=NODES), scalar=scale,
                    in1=sbias[par][:, s, :].unsqueeze(1).to_broadcast([P, HEADS, NODES]), op0=ALU.mult, op1=ALU.add,
                ).then_inc(dve_sc, 1)
                dve.wait_ge(dve_sc, n + 1)
                if counted(n - 1):
                    dve.wait_ge(pool_p, n - 1)
                nc.vector.tensor_reduce(st[b][:, 0, :], sc[b][:, :, :], AX.X, ALU.max).then_inc(dve_mx, 1)
                if wo:
                    nc.vector.tensor_reduce(st[b][:, 1, :], sc[b][:, :, :], AX.X, ALU.min).then_inc(dve_mn, 1)

            def softmax_sum(n, s):
                b = s % 2
                dve.wait_ge(act_e, n + 1)
                nc.vector.tensor_reduce(st[b][:, 2, :], pr[b][:, :, :], AX.X, ALU.add).then_inc(dve_sum, 1)
                if wo:
                    dve.wait_ge(dve_mn, n + 1)
                    dve.wait_ge(dve_mx, n + 1)
                    nc.vector.scalar_tensor_tensor(out=st[b][:, 3, :], in0=st[b][:, 1, :], scalar=-1.0, in1=st[b][:, 0, :],
                                                   op0=ALU.mult, op1=ALU.max).then_inc(dve_m0, 1)
                    dve.wait_ge(dve_sum, n + 1)
                    nc.vector.reciprocal(st[b][:, 4, :], st[b][:, 2, :]).then_inc(dve_inv, 1)
                    dve.wait_ge(dve_inv, n + 1)
                    dve.wait_ge(dve_m0, n + 1)
                    nc.vector.scalar_tensor_tensor(out=st[b][:, 5, :], in0=st[b][:, 3, :], scalar=0.0, in1=st[b][:, 4, :],
                                                   op0=ALU.not_equal, op1=ALU.mult).then_inc(dve_rinv, 1)
                else:
                    dve.wait_ge(dve_sum, n + 1)
                    nc.vector.reciprocal(st[b][:, 5, :], st[b][:, 2, :]).then_inc(dve_rinv, 1)

            def low_part(n, b):
                if not inside(n, units) or not wo:
                    return
                dve.wait_ge(act_o, n + 1)
                nc.vector.tensor_tensor(oT[b][:, 1, :, :], ps_o[:, :D].rearrange("p (t q) -> p t q", q=P),
                                        oT[b][:, 0, :, :].bitcast(F32), ALU.subtract).then_inc(dve_o, 1)

            def residual(n, count, b):
                if not inside(n, units):
                    return
                dve.wait_ge(pe_y, n + 1)
                dve.wait_ge(s_xr[b], 16 * (count + 1))
                nc.vector.tensor_tensor(res[b][:, :], ps_y[:, :D], xr[b][:, :], ALU.add).then_inc(dve_res, 1)
                dve.wait_ge(dve_res, n + 1)
                nc.vector.bn_stats(ln[b][:, 0:6], res[b][:, :]).then_inc(dve_bn, 1)
                dve.wait_ge(c_zero, 1)
                dve.wait_ge(dve_bn, n + 1)
                nc.vector.bn_aggr(ln[b][:, 6:8], ln[b][:, 0:6]).then_inc(dve_mv, 1)

            def normed(n, count, b):
                if not inside(n, units):
                    return
                dve.wait_ge(pool_rs, n + 1)
                dve.wait_ge(dve_mv, n + 1)
                if counted(16 * count):
                    dve.wait_ge(s_out[b], 16 * count)
                nc.vector.tensor_scalar(yo[b][:, :], res[b][:, :], ln[b][:, 6:7], ln[b][:, 9:10], ALU.subtract,
                                        ALU.mult).then_inc(dve_y, 1)

            if row_bias_cols or beta is not None:
                dve.wait_ge(s_small, 16 * n_small)
            rows_T(0, 0)
            edges(0, 0, 0)
            spread(0, 0, 0, 0)
            rows_T(1, 1)
            ni = [0]

            def group(i, pair, par):
                ni[0] = i
                for s in range(UNITS):
                    n = i * UNITS + s
                    count = pair * 4 + 2 * par + s // 2 - 1
                    residual(n - 2, count, s % 2)
                    softmax_max(n, par, s)
                    normed(n - 2, count, s % 2)
                    if s < UNITS - 1:
                        spread(n + 1, i, par, s + 1)
                    else:
                        spread(n + 1, i + 1, 1 - par, 0)
                    if s == 2:
                        edges(i + 1, pair + (1 if par else 0), 1 - par)
                    softmax_sum(n, s)
                    low_part(n - 1, (s - 1) % 2)
                    if s == UNITS - 1:
                        rows_T(i + 2, par)

            over_groups(dve, groups, group)
            low_part(units - 1, 1)
            for n in (units - 2, units - 1):
                residual(n, n // 2, n % 2)
                normed(n, n // 2, n % 2)

    nc.clear_and_free_semaphores(a.sems)
    nc.all_engine_barrier()


def digcn_pass(nc, tag, src, dst, adj, mats, row_biases, ln_scale, ln_shift, residual_src, groups):
    units = groups * UNITS
    LEFT, RIGHT, SELF = range(3)
    src_g = src.rearrange("(i u p) d -> i p u d", u=UNITS, p=P)
    adj_g = adj.rearrange("(i u p) k -> i p u k", u=UNITS, p=P)
    dst_u = dst.rearrange("(i u p) d -> i u p d", u=UNITS, p=P)
    ends = residual_src is not None
    if ends:
        res_u = residual_src.rearrange("(i u p) d -> i u p d", u=UNITS, p=P)

    with ExitStack() as ctx:
        a = Pass(nc, ctx, tag)
        W = [a.sb(f"w{m}", [P, 2, KT, D], F32R) for m in range(3)]
        raw = [a.sb(f"raw{m}", [P, KT, D]) for m in range(2)]
        ident = a.sb("ident", [P, P])
        ones = a.sb("ones", [P, P])
        pick = a.sb("pick", [P, P], F32R)
        brow = a.sb("brow", [P, 3, D])
        bround = a.sb("bround", [P, 3, D], F32R)
        bias = a.sb("bias", [P, 3, D], F32R)
        gain = a.sb("gain", [P, D])
        shift = a.sb("shift", [P, D])
        mhalf = a.sb("mhalf", [P, 1])
        epst = a.sb("epst", [P, 1])
        epsi = a.sb("epsi", [P, 1])
        after = a.sb("after", [P, P])
        before = a.sb("before", [P, P])
        same = a.sb("same", [P, NODES])
        xa = a.sb("xa", [P, UNITS, D])
        hT = [a.sb(f"hT{b}", [P, 2, KT, ROWS], F32R) for b in range(2)]
        edge = [a.sb(f"edge{b}", [P, UNITS, NODES]) for b in range(2)]
        half = a.sb("half", [P, UNITS, NODES])
        u0 = a.sb("u0", [P, UNITS, NODES])
        u1 = a.sb("u1", [P, UNITS, NODES])
        u2 = a.sb("u2", [P, UNITS, NODES])
        u3 = a.sb("u3", [P, UNITS, NODES])
        u4 = a.sb("u4", [P, UNITS, NODES])
        u5 = a.sb("u5", [P, UNITS, NODES])
        u6 = a.sb("u6", [P, UNITS, NODES])
        st = a.sb("st", [P, 6, UNITS])
        diag = [a.sb(f"diag{b}", [P, UNITS]) for b in range(2)]
        wide = a.sb("wide", [P, UNITS, P])
        part = [a.sb(f"part{m}", [P, UNITS, P]) for m in range(2)]
        aT = [a.sb(f"aT{b}", [P, 2, 2, UNITS, P], F32R) for b in range(2)]
        hp = [a.sb(f"hp{b}", [P, 2, 2, D], F32R) for b in range(2)]
        hs = [a.sb(f"hs{b}", [P, D]) for b in range(2)]
        c0 = [a.sb(f"c0{b}", [P, D]) for b in range(2)]
        c1 = [a.sb(f"c1{b}", [P, D]) for b in range(2)]
        c2 = [a.sb(f"c2{b}", [P, D]) for b in range(2)]
        ln = [a.sb(f"ln{b}", [P, 20]) for b in range(2)]
        xr = [a.sb(f"xr{b}", [P, D]) for b in range(2)]
        c3 = [a.sb(f"c3{b}", [P, D]) for b in range(2)]
        yo = [a.sb(f"yo{b}", [P, D]) for b in range(2)]

        ps_h = [a.ps(f"ps_h{m}", [P, 512]) for m in range(3)]
        ps_c = a.ps("ps_c", [P, 512])
        ps_u = a.ps("ps_u", [P, 2 * 512])
        ps_a = a.ps("ps_a", [P, 512])
        ps_x = a.ps("ps_x", [P, 512])

        s_raw = [a.sem(f"s_raw{b}") for b in range(2)]
        s_edge = [a.sem(f"s_edge{b}") for b in range(2)]
        s_xr = [a.sem(f"s_xr{b}") for b in range(2)]
        s_out = [a.sem(f"s_out{b}") for b in range(2)]
        s_small, s_xa, c_ident, c_zero, c_one, c_row, c_mask = (
            a.sem(x) for x in ("s_small", "s_xa", "c_ident", "c_zero", "c_one", "c_row", "c_mask"))
        pe_w, act_w, dve_w = a.sem("pe_w"), a.sem("act_w"), a.sem("dve_w")
        pe_x, pe_h, pe_u, pe_a, pe_c = (a.sem(x) for x in ("pe_x", "pe_h", "pe_u", "pe_a", "pe_c"))
        act_x, act_h, act_half, act_e, act_a, act_y = (
            a.sem(x) for x in ("act_x", "act_h", "act_half", "act_e", "act_a", "act_y"))
        dve_x, dve_h, dve_u, dve_mx, dve_sum, dve_inv, dve_dsum, dve_deps, dve_rs, dve_attn, dve_wide, dve_dg, dve_part = (
            a.sem(x) for x in ("dve_x", "dve_h", "dve_u", "dve_mx", "dve_sum", "dve_inv", "dve_dsum", "dve_deps",
                               "dve_rs", "dve_attn", "dve_wide", "dve_dg", "dve_part"))
        dve_c, dve_bn, dve_mv, dve_g, dve_o, dve_r, dve_bn2, dve_mv2, dve_y = (
            a.sem(x) for x in ("dve_c", "dve_bn", "dve_mv", "dve_g", "dve_o", "dve_r", "dve_bn2", "dve_mv2", "dve_y"))
        pool_sub, pool_p, pool_d, pool_pick, pool_a, pool_ve, pool_rs, pool_ve2, pool_rs2 = (
            a.sem(x) for x in ("pool_sub", "pool_p", "pool_d", "pool_pick", "pool_a", "pool_ve", "pool_rs", "pool_ve2", "pool_rs2"))

        n_small = 3 * 2 + 2
        steps = 3 * KT
        zeros = 3
        masks = 3
        rows_ready = 2 + 3 * 2
        items = {LEFT: 0, RIGHT: 1, SELF: 2}

        block = ctx.enter_context(nc.Block())

        @block.sync
        def _(sp):
            for m in range(3):
                if m >= 2:
                    if counted(KT * (m - 1)):
                        sp.wait_ge(dve_w, KT * (m - 1))
                sp.dma_start(raw[m % 2][:, :, :], mats[m].rearrange("(t p) n -> p t n", p=P)).then_inc(s_raw[m % 2], 16)
                if m == 1:
                    sp.dma_start(xa[:, :, :], src_g[0]).then_inc(s_xa, 16)
                    sp.dma_start(edge[0][:, :, :], adj_g[0]).then_inc(s_edge[0], 16)
                    for j, b in enumerate(row_biases):
                        for row in (0, 32):
                            sp.dma_start(brow[row:row + 1, j, :], b).then_inc(s_small, 16)
                    sp.dma_start(gain[:, :], ln_scale.to_broadcast([P, D])).then_inc(s_small, 16)
                    sp.dma_start(shift[:, :], ln_shift.to_broadcast([P, D])).then_inc(s_small, 16)
            sp.wait_ge(pe_x, KT)
            sp.dma_start(xa[:, :, :], src_g[1]).then_inc(s_xa, 16)

            def store(n, i, s):
                if inside(n, units):
                    sp.wait_ge(dve_y if ends else act_y, n + 1)
                    sp.dma_start(dst_u[i, s], yo[s % 2][:, :]).then_inc(s_out[s % 2], 16)

            def group(i, pair, par):
                for s in range(UNITS):
                    n = i * UNITS + s
                    if s == 1 and inside(i + 1, groups):
                        if counted(i):
                            sp.wait_ge(pool_d, i)
                        sp.dma_start(edge[1 - par][:, :, :], adj_g[i + 1]).then_inc(s_edge[1 - par], 16)
                    if s == 1 and inside(i + 2, groups):
                        sp.wait_ge(pe_x, KT * (i + 2))
                        sp.dma_start(xa[:, :, :], src_g[i + 2]).then_inc(s_xa, 16)
                    if ends:
                        if counted(n - 1):
                            sp.wait_ge(dve_r, n - 1)
                        sp.dma_start(xr[s % 2][:, :], res_u[i, s]).then_inc(s_xr[s % 2], 16)
                    if s >= 2:
                        store(n - 2, i, s - 2)
                    else:
                        store(n - 2, i - 1, s + 2)

            over_groups(sp, groups, group)
            store(units - 2, groups - 1, 2)
            store(units - 1, groups - 1, 3)
            for b in range(2):
                sp.wait_ge(s_out[b], 16 * (units // 2))

        @block.gpsimd
        def _(pool):
            nc.gpsimd.memset(ones[:, :], 1.0).then_inc(c_one, 1)
            nc.gpsimd.memset(mhalf[:, :], -0.5).then_inc(c_one, 1)
            nc.gpsimd.memset(epst[:, :], LN_EPS).then_inc(c_one, 1)
            nc.gpsimd.memset(epsi[:, :], LN_EPS_INNER).then_inc(c_one, 1)
            pool.wait_ge(c_one, 4)
            nc.gpsimd.affine_select(out=ident[:, :], in_=ones[:, :], compare_op=ALU.is_equal, fill=0.0,
                                    base=0, pattern=[[-1, P]], channel_multiplier=1).then_inc(c_ident, 1)
            nc.gpsimd.affine_select(out=after[:, :], in_=ones[:, :], compare_op=ALU.is_gt, fill=0.0,
                                    base=0, pattern=[[-1, P]], channel_multiplier=1).then_inc(c_mask, 1)
            nc.gpsimd.affine_select(out=before[:, :], in_=ones[:, :], compare_op=ALU.is_gt, fill=0.0,
                                    base=0, pattern=[[1, P]], channel_multiplier=-1).then_inc(c_mask, 1)
            pool.wait_ge(c_ident, 1)
            nc.gpsimd.tensor_tensor(same[:, :], ident[:, 0:NODES], ident[:, NODES:P], ALU.add).then_inc(c_mask, 1)

            def attention(g, gpar, step):
                if not inside(g, groups):
                    return
                if step == 0:
                    pool.wait_ge(dve_mx, g + 1)
                    nc.gpsimd.tensor_tensor(u1[:, :, :], u0[:, :, :], st[:, 0, :].unsqueeze(2).to_broadcast([P, UNITS, NODES]),
                                            ALU.subtract).then_inc(pool_sub, 1)
                elif step == 1:
                    pool.wait_ge(dve_inv, g + 1)
                    nc.gpsimd.tensor_tensor(u3[:, :, :], u2[:, :, :], st[:, 2, :].unsqueeze(2).to_broadcast([P, UNITS, NODES]),
                                            ALU.mult).then_inc(pool_p, 1)
                    pool.wait_ge(pool_p, g + 1)
                    pool.wait_ge(s_edge[gpar], 16 * (gpair(g, gpar) + 1))
                    nc.gpsimd.tensor_tensor(u4[:, :, :], u3[:, :, :], edge[gpar][:, :, :], ALU.mult).then_inc(pool_d, 1)
                elif step == 2:
                    pool.wait_ge(dve_attn, g + 1)
                    pool.wait_ge(c_mask, masks)
                    nc.gpsimd.tensor_tensor(u6[:, :, :], u5[:, :, :], same[:, :].unsqueeze(1).to_broadcast([P, UNITS, NODES]),
                                            ALU.mult).then_inc(pool_pick, 1)
                else:
                    for m in range(2):
                        pool.wait_ge(act_a, 2 * g + m + 1)
                        nc.gpsimd.tensor_tensor(aT[gpar][:, m, 1, :, :], part[m][:, :, :],
                                                aT[gpar][:, m, 0, :, :].bitcast(F32), ALU.subtract).then_inc(pool_a, 1)

            def gpair(g, gpar):
                return g // 2 if isinstance(g, int) else pi[0] + (1 if gpar == 0 else 0)

            pi = [0]

            def rstd(n, b, eps, at, ready, ve, rs):
                if inside(n, units):
                    pool.wait_ge(ready, n + 1)
                    nc.gpsimd.tensor_tensor(ln[b][:, at + 2:at + 3], ln[b][:, at + 1:at + 2], eps[:, :], ALU.add).then_inc(ve, 1)
                    pool.wait_ge(ve, n + 1)
                    nc.gpsimd.tensor_tensor(ln[b][:, at + 3:at + 4], ln[b][:, at + 2:at + 3], mhalf[:, :], ALU.pow).then_inc(rs, 1)

            for step in range(4):
                attention(0, 0, step)

            def group(i, pair, par):
                pi[0] = pair
                for s in range(UNITS):
                    n = i * UNITS + s
                    rstd(n - 1, (s - 1) % 2, epsi, 6, dve_mv, pool_ve, pool_rs)
                    if ends:
                        rstd(n - 2, s % 2, epst, 16, dve_mv2, pool_ve2, pool_rs2)
                    if s:
                        attention(i + 1, 1 - par, s - 1)
                    if s == 3:
                        attention(i + 1, 1 - par, 3)

            over_groups(pool, groups, group)
            rstd(units - 1, 1, epsi, 6, dve_mv, pool_ve, pool_rs)
            if ends:
                rstd(units - 2, 0, epst, 16, dve_mv2, pool_ve2, pool_rs2)
                rstd(units - 1, 1, epst, 16, dve_mv2, pool_ve2, pool_rs2)

        @block.tensor
        def _(pe):
            pe.wait_ge(c_ident, 1)
            for m in range(3):
                pe.wait_ge(s_raw[m % 2], 16 * (m // 2 + 1))
                for t in range(KT):
                    step = m * KT + t
                    if counted(step - 1):
                        pe.wait_ge(dve_w, step - 1)
                    for o in range(KT):
                        last = nc.tensor.transpose(ps_h[step % 2][:, o * P:(o + 1) * P],
                                                   raw[m % 2][:, o, t * P:(t + 1) * P], ident[:, :])
                    last.then_inc(pe_w, 1)

            def rows_T(g):
                if not inside(g, groups):
                    return
                pe.wait_ge(s_xa, 16 * (g + 1))
                for t in range(KT):
                    if counted(KT * g + t):
                        pe.wait_ge(dve_x, KT * g + t)
                    for u in range(UNITS):
                        last = nc.tensor.transpose(ps_x[:, u * P:(u + 1) * P], xa[:, u, t * P:(t + 1) * P], ident[:, :])
                    last.then_inc(pe_x, 1)

            def products(g, gpar):
                if not inside(g, groups):
                    return
                pe.wait_ge(act_x, KT * (g + 1))
                pe.wait_ge(dve_x, KT * (g + 1))
                if counted(2 * g):
                    pe.wait_ge(dve_u, 2 * g)
                for u in range(UNITS):
                    q = slice(u * P, (u + 1) * P)
                    for c in range(2):
                        for t in range(KT):
                            last = nc.tensor.matmul(ps_u[:, u * 256:(u + 1) * 256], hT[gpar][:, c, t, q],
                                                    hT[gpar][:, :, t, q], start=c + t == 0, stop=c == 1 and t == KT - 1)
                last.then_inc(pe_u, 1)

            def attention_T(g):
                if not inside(g, groups):
                    return
                pe.wait_ge(dve_wide, 2 * (g + 1))
                if counted(2 * g):
                    pe.wait_ge(dve_part, 2 * g)
                for u in range(UNITS):
                    last = nc.tensor.transpose(ps_a[:, u * P:(u + 1) * P], wide[:, u, :], ident[:, :])
                last.then_inc(pe_a, 1)

            def project(n, gpar, s, m):
                if m == SELF:
                    if counted(3 * n):
                        pe.wait_ge(act_h, 3 * n)
                else:
                    if counted(2 * (n - 1) + m + 1):
                        pe.wait_ge(dve_h, 2 * (n - 1) + m + 1)
                for c, (l, r) in enumerate(SPLIT):
                    for t in range(KT):
                        nc.tensor.matmul(ps_h[m][:, :D], hT[gpar][:, l, t, s * P:(s + 1) * P], W[m][:, r, t, :],
                                         start=c + t == 0, stop=False)
                nc.tensor.matmul(ps_h[m][:, :D], pick[:, :], bias[:, m, :], start=False, stop=True).then_inc(pe_h, 1)

            def context(n, gpar, s):
                if not inside(n, units):
                    return
                if counted(3 * (n + 1) - 1):
                    pe.wait_ge(act_h, 3 * (n + 1) - 1)
                pe.wait_ge(dve_h, 2 * (n + 1))
                if counted(ga[0]):
                    pe.wait_ge(pool_a, ga[0])
                if counted(n):
                    pe.wait_ge(dve_c, n)
                for m in range(2):
                    for c, (l, r) in enumerate(SPLIT):
                        last = nc.tensor.matmul(ps_c[:, :D], aT[gpar][:, m, l, s, :], hp[s % 2][:, m, r, :],
                                                start=m + c == 0, stop=m == 1 and c == 2)
                last.then_inc(pe_c, 1)

            ga = [0]
            pe.wait_ge(act_w, steps)
            pe.wait_ge(dve_w, steps)
            rows_T(0)
            products(0, 0)
            pe.wait_ge(c_zero, zeros)
            attention_T(0)
            pe.wait_ge(c_row, rows_ready)

            def group(i, pair, par):
                for s in range(UNITS):
                    n = i * UNITS + s
                    if s:
                        ppar, ps, ga[0] = par, s - 1, 2 * (i + 1)
                    else:
                        ppar, ps, ga[0] = 1 - par, UNITS - 1, 2 * i
                    project(n, par, s, LEFT)
                    if s == 0:
                        rows_T(i + 1)
                    if s == 1:
                        products(i + 1, 1 - par)
                    context(n - 1, ppar, ps)
                    project(n, par, s, RIGHT)
                    project(n, par, s, SELF)
                    if s == 3:
                        attention_T(i + 1)

            over_groups(pe, groups, group)
            ga[0] = 2 * groups
            context(units - 1, 1, UNITS - 1)

        @block.scalar
        def _(act):
            for step in range(steps):
                m, t = divmod(step, KT)
                act.wait_ge(pe_w, step + 1)
                nc.scalar.activation(W[m][:, 0, t, :], ps_h[step % 2][:, :D], ACT.Copy).then_inc(act_w, 1)
            act.wait_ge(s_small, 16 * n_small)
            act.wait_ge(c_zero, zeros)
            for j in range(3):
                nc.scalar.activation(bias[0:1, j, :], brow[0:1, j, :], ACT.Copy).then_inc(c_row, 1)
                nc.scalar.activation(bround[32:33, j, :], brow[32:33, j, :], ACT.Copy).then_inc(act_w, 1)

            def rows_T(g, gpar):
                if not inside(g, groups):
                    return
                for t in range(KT):
                    act.wait_ge(pe_x, KT * g + t + 1)
                    nc.scalar.activation(hT[gpar][:, 0, t, :], ps_x[:, :], ACT.Copy).then_inc(act_x, 1)

            def attention(g, gpar, step):
                if not inside(g, groups):
                    return
                if step == 0:
                    act.wait_ge(pe_u, g + 1)
                    if counted(2 * g):
                        act.wait_ge(dve_u, 2 * g)
                    for b in range(GPU):
                        q = slice(b * NODES, (b + 1) * NODES)
                        nc.scalar.activation(half[q, :, :], ps_u[q, :].rearrange("p (u c) -> p u c", u=UNITS)[
                            :, :, P + b * NODES:P + (b + 1) * NODES], ACT.Copy).then_inc(act_half, 1)
                elif step == 1:
                    act.wait_ge(pool_sub, g + 1)
                    nc.scalar.activation(u2[:, :, :], u1[:, :, :], ACT.Exp, scale=float(D) ** -0.5).then_inc(act_e, 1)
                else:
                    for m in range(2):
                        act.wait_ge(dve_part, 2 * g + m + 1)
                        nc.scalar.activation(aT[gpar][:, m, 0, :, :], part[m][:, :, :], ACT.Copy).then_inc(act_a, 1)

            def left_right(n, b, m):
                act.wait_ge(pe_h, 3 * n + m + 1)
                if counted(n - 1):
                    act.wait_ge(pe_c, n - 1)
                nc.scalar.activation(hp[b][:, m, 0, :], ps_h[m][:, :D], ACT.Copy).then_inc(act_h, 1)

            def relu(n, count, b):
                if inside(n, units) and not ends:
                    act.wait_ge(dve_o, n + 1)
                    if counted(16 * count):
                        act.wait_ge(s_out[b], 16 * count)
                    nc.scalar.activation(yo[b][:, :], c2[b][:, :], ACT.Relu).then_inc(act_y, 1)

            rows_T(0, 0)
            for step in range(3):
                attention(0, 0, step)

            def group(i, pair, par):
                for s in range(UNITS):
                    n, b = i * UNITS + s, s % 2
                    left_right(n, b, LEFT)
                    if s == 0:
                        rows_T(i + 1, 1 - par)
                    if s == 1:
                        attention(i + 1, 1 - par, 0)
                    if s == 2:
                        attention(i + 1, 1 - par, 1)
                    left_right(n, b, RIGHT)
                    relu(n - 2, pair * 4 + 2 * par + s // 2 - 1, b)
                    act.wait_ge(pe_h, 3 * n + 3)
                    act.wait_ge(dve_dg, i + 1)
                    if counted(n - 1):
                        act.wait_ge(dve_c, n - 1)
                    nc.scalar.activation(hs[b][:, :], ps_h[SELF][:, :D], ACT.Copy, scale=diag[par][:, s:s + 1]).then_inc(act_h, 1)
                    if s == 3:
                        attention(i + 1, 1 - par, 2)

            over_groups(act, groups, group)
            relu(units - 2, units // 2 - 1, 0)
            relu(units - 1, units // 2 - 1, 1)

        @block.vector
        def _(dve):
            nc.vector.memset(pick[:, :].bitcast(F32), 0.0).then_inc(c_zero, 1)
            nc.vector.memset(bias[:, :, :].bitcast(F32), 0.0).then_inc(c_zero, 1)
            nc.vector.memset(wide[:, :, :], 0.0).then_inc(c_zero, 1)
            dve.wait_ge(c_one, 1)
            dve.wait_ge(c_zero, zeros)
            for row in (0, 32):
                nc.vector.tensor_copy(pick[row:row + 1, :], ones[row:row + 1, :]).then_inc(c_row, 1)
            for step in range(steps):
                m, t = divmod(step, KT)
                dve.wait_ge(act_w, step + 1)
                nc.vector.tensor_tensor(W[m][:, 1, t, :], ps_h[step % 2][:, :D], W[m][:, 0, t, :].bitcast(F32),
                                        ALU.subtract).then_inc(dve_w, 1)
            dve.wait_ge(act_w, steps + 3)
            dve.wait_ge(s_small, 16 * n_small)
            for j in range(3):
                nc.vector.tensor_tensor(bias[32:33, j, :], brow[32:33, j, :], bround[32:33, j, :].bitcast(F32),
                                        ALU.subtract).then_inc(c_row, 1)
            dve.wait_ge(c_mask, masks)

            def rows_T(g, gpar):
                if not inside(g, groups):
                    return
                for t in range(KT):
                    dve.wait_ge(act_x, KT * g + t + 1)
                    nc.vector.tensor_tensor(hT[gpar][:, 1, t, :], ps_x[:, :], hT[gpar][:, 0, t, :].bitcast(F32),
                                            ALU.subtract).then_inc(dve_x, 1)

            def attention(g, gpar, step):
                if not inside(g, groups):
                    return
                if step == 0:
                    dve.wait_ge(act_half, 2 * (g + 1))
                    dve.wait_ge(pool_sub, g)
                    for b in range(GPU):
                        q = slice(b * NODES, (b + 1) * NODES)
                        nc.vector.tensor_tensor(u0[q, :, :], ps_u[q, :].rearrange("p (u c) -> p u c", u=UNITS)[
                            :, :, b * NODES:(b + 1) * NODES], half[q, :, :], ALU.add).then_inc(dve_u, 1)
                    dve.wait_ge(dve_u, 2 * (g + 1))
                    nc.vector.tensor_reduce(st[:, 0, :], u0[:, :, :], AX.X, ALU.max).then_inc(dve_mx, 1)
                elif step == 1:
                    dve.wait_ge(act_e, g + 1)
                    nc.vector.tensor_reduce(st[:, 1, :], u2[:, :, :], AX.X, ALU.add).then_inc(dve_sum, 1)
                    dve.wait_ge(dve_sum, g + 1)
                    nc.vector.reciprocal(st[:, 2, :], st[:, 1, :]).then_inc(dve_inv, 1)
                elif step == 2:
                    dve.wait_ge(pool_d, g + 1)
                    nc.vector.tensor_reduce(st[:, 3, :], u4[:, :, :], AX.X, ALU.add).then_inc(dve_dsum, 1)
                    dve.wait_ge(dve_dsum, g + 1)
                    nc.vector.tensor_scalar(st[:, 4, :], st[:, 3, :], 1e-10, 0.0, ALU.add, ALU.add).then_inc(dve_deps, 1)
                    dve.wait_ge(dve_deps, g + 1)
                    nc.vector.reciprocal(st[:, 5, :], st[:, 4, :]).then_inc(dve_rs, 1)
                    dve.wait_ge(dve_rs, g + 1)
                    dve.wait_ge(pe_a, g)
                    dve.wait_ge(pool_pick, g)
                    nc.vector.tensor_tensor(u5[:, :, :], u4[:, :, :], st[:, 5, :].unsqueeze(2).to_broadcast([P, UNITS, NODES]),
                                            ALU.mult).then_inc(dve_attn, 1)
                    dve.wait_ge(dve_attn, g + 1)
                    for b in range(GPU):
                        q = slice(b * NODES, (b + 1) * NODES)
                        nc.vector.tensor_copy(wide[q, :, b * NODES:(b + 1) * NODES], u5[q, :, :]).then_inc(dve_wide, 1)
                else:
                    dve.wait_ge(pool_pick, g + 1)
                    nc.vector.tensor_reduce(diag[gpar][:, :], u6[:, :, :], AX.X, ALU.add).then_inc(dve_dg, 1)
                    dve.wait_ge(pe_a, g + 1)
                    if counted(2 * g):
                        dve.wait_ge(pool_a, 2 * g)
                    for m, mask in enumerate((after, before)):
                        nc.vector.tensor_tensor(part[m][:, :, :], ps_a[:, :].rearrange("p (u q) -> p u q", u=UNITS),
                                                mask[:, :].unsqueeze(1).to_broadcast([P, UNITS, P]), ALU.mult).then_inc(dve_part, 1)

            def left_right(n, b, m):
                dve.wait_ge(act_h, 3 * n + m + 1)
                nc.vector.tensor_tensor(hp[b][:, m, 1, :], ps_h[m][:, :D], hp[b][:, m, 0, :].bitcast(F32),
                                        ALU.subtract).then_inc(dve_h, 1)

            def context(n, b):
                if not inside(n, units):
                    return
                dve.wait_ge(pe_c, n + 1)
                dve.wait_ge(act_h, 3 * (n + 1))
                nc.vector.tensor_tensor(c0[b][:, :], ps_c[:, :D], hs[b][:, :], ALU.add).then_inc(dve_c, 1)
                dve.wait_ge(dve_c, n + 1)
                nc.vector.bn_stats(ln[b][:, 0:6], c0[b][:, :]).then_inc(dve_bn, 1)
                dve.wait_ge(c_zero, 1)
                dve.wait_ge(dve_bn, n + 1)
                nc.vector.bn_aggr(ln[b][:, 6:8], ln[b][:, 0:6]).then_inc(dve_mv, 1)

            def inner_norm(n, count, b):
                if not inside(n, units):
                    return
                dve.wait_ge(dve_mv, n + 1)
                nc.vector.scalar_tensor_tensor(out=c1[b][:, :], in0=c0[b][:, :], scalar=ln[b][:, 6:7], in1=gain[:, :],
                                               op0=ALU.subtract, op1=ALU.mult).then_inc(dve_g, 1)
                dve.wait_ge(dve_g, n + 1)
                dve.wait_ge(pool_rs, n + 1)
                if not ends:
                    if counted(n - 1):
                        dve.wait_ge(act_y, n - 1)
                nc.vector.scalar_tensor_tensor(out=c2[b][:, :], in0=c1[b][:, :], scalar=ln[b][:, 9:10], in1=shift[:, :],
                                               op0=ALU.mult, op1=ALU.add).then_inc(dve_o, 1)
                if ends:
                    dve.wait_ge(dve_o, n + 1)
                    dve.wait_ge(s_xr[b], 16 * (count + 1))
                    nc.vector.scalar_tensor_tensor(out=c3[b][:, :], in0=c2[b][:, :], scalar=0.0, in1=xr[b][:, :],
                                                   op0=ALU.max, op1=ALU.add).then_inc(dve_r, 1)
                    dve.wait_ge(dve_r, n + 1)
                    nc.vector.bn_stats(ln[b][:, 10:16], c3[b][:, :]).then_inc(dve_bn2, 1)
                    dve.wait_ge(c_zero, 1)
                    dve.wait_ge(dve_bn2, n + 1)
                    nc.vector.bn_aggr(ln[b][:, 16:18], ln[b][:, 10:16]).then_inc(dve_mv2, 1)

            def normed(n, count, b):
                if not inside(n, units) or not ends:
                    return
                dve.wait_ge(pool_rs2, n + 1)
                if counted(16 * count):
                    dve.wait_ge(s_out[b], 16 * count)
                nc.vector.tensor_scalar(yo[b][:, :], c3[b][:, :], ln[b][:, 16:17], ln[b][:, 19:20], ALU.subtract,
                                        ALU.mult).then_inc(dve_y, 1)

            rows_T(0, 0)
            for step in range(4):
                attention(0, 0, step)

            def group(i, pair, par):
                for s in range(UNITS):
                    n, b = i * UNITS + s, s % 2
                    left_right(n, b, LEFT)
                    if s == 0:
                        rows_T(i + 1, 1 - par)
                    context(n - 1, 1 - b)
                    normed(n - 2, pair * 4 + 2 * par + s // 2 - 1, b)
                    if s:
                        attention(i + 1, 1 - par, s - 1)
                    left_right(n, b, RIGHT)
                    inner_norm(n - 1, pair * 4 + 2 * par + (s + 1) // 2 - 1, 1 - b)
                    if s == 3:
                        attention(i + 1, 1 - par, 3)

            over_groups(dve, groups, group)
            context(units - 1, 1)
            normed(units - 2, units // 2 - 1, 0)
            inner_norm(units - 1, units // 2 - 1, 1)
            normed(units - 1, units // 2 - 1, 1)

    nc.clear_and_free_semaphores(a.sems)
    nc.all_engine_barrier()


def graph_layers(nc, ins, out):
    def flat(name):
        return ins[name].rearrange("b n d -> (b n) d")

    x, adj = flat("x"), flat("adj")
    groups = x.shape[0] // ROWS
    kept = [nc.dram_tensor(f"rows{k}", (x.shape[0], D), F32, kind="Internal").ap() for k in range(4)]
    y = out.rearrange("b n d -> (b n) d")
    l0, l1, l2, l3 = (lambda k, layer=layer: ins[f"L{layer}_gnn_{k}"] for layer in range(4))

    attention_pass(nc, "l0", x, kept[0], adj, ([l0(k) for k in ("Wq", "Wk", "Wv", "Wo")], None), float(D) ** -0.5,
                   True, True, l0("bv"), l0("bo"), None, 2.0, groups)
    attention_pass(nc, "l1", kept[0], kept[1], adj, ([l1(k) for k in ("Wq", "Wk", "Wv")], (l1("bq"), l1("bk"))),
                   float(D // HEADS) ** -0.5, False, False, l1("bv"), None, l1("beta"), None, groups)
    for k in range(2):
        digcn_pass(nc, f"l2{k}", kept[1 + k], kept[2 + k], adj, [l2(m)[k] for m in ("Wl", "Wr", "Ws")],
                   [l2(m)[k:k + 1, :] for m in ("bl", "br", "bs")], l2("ln_w")[k:k + 1, :], l2("ln_b")[k:k + 1, :],
                   kept[1] if k else None, groups)
    attention_pass(nc, "l3", kept[3], y, adj, ([l3(k) for k in ("Wq", "Wk", "Wv", "Wo")], None), float(D) ** -0.5,
                   True, True, l3("bv"), l3("bo"), None, 1.0, groups)


_INS = (["x", "adj"] + [f"L0_gnn_{k}" for k in ("Wq", "Wk", "Wv", "bv", "Wo", "bo")]
        + [f"L1_gnn_{k}" for k in ("Wq", "bq", "Wk", "bk", "Wv", "bv", "beta")]
        + [f"L2_gnn_{k}" for k in ("Wl", "bl", "Ws", "bs", "Wr", "br", "ln_w", "ln_b")]
        + [f"L3_gnn_{k}" for k in ("Wq", "Wk", "Wv", "bv", "Wo", "bo")])


def kernel(**inputs):
    import numpy as np
    import concourse.bacc as bacc
    from concourse.bass_utils import run_bass_kernel_spmd

    nc = bacc.Bacc("TRN2", target_bir_lowering=False, num_devices=1)
    arrays, ins = {}, {}
    for name in _INS:
        a = np.ascontiguousarray(inputs[name])
        if a.ndim == 0:
            a = a.reshape(1)
        arrays[f"in_{name}"] = a
        ins[name] = nc.dram_tensor(f"in_{name}", a.shape, mybir.dt.from_np(a.dtype), kind="ExternalInput").ap()
    out = nc.dram_tensor("out", tuple(inputs["x"].shape), F32, kind="ExternalOutput").ap()
    graph_layers(nc, ins, out)
    return run_bass_kernel_spmd(nc, [arrays], core_ids=[0]).results[0]["out"]
```

```python
from contextlib import ExitStack

import concourse.bass as bass
from concourse import mybir

F32 = mybir.dt.float32
F32R = mybir.dt.float32r
ALU = mybir.AluOpType
ACT = mybir.ActivationFunctionType
AX = mybir.AxisListType

P = 128
NODES = 64
D = 384
KT = D // P
HEADS = 12
PAIRS = HEADS // 2
GPU = P // NODES
UNITS = 4
ROWS = P * UNITS
LN_EPS = 1e-5
LN_EPS_INNER = 1e-12
MASKED = -9000000000000000.0
SPLIT = ((0, 0), (1, 0), (0, 1))


def counted(value):
    return not isinstance(value, int) or value > 0


def inside(index, count):
    return not isinstance(index, int) or 0 <= index < count


def over_groups(eng, groups, group):
    pairs = groups // 2
    for par in range(2):
        group(par, 0, par)
    with eng.Fori(1, pairs - 1) as pair:
        for par in range(2):
            group(pair * 2 + par, pair, par)
    for par in range(2):
        group(groups - 2 + par, pairs - 1, par)


class Shared:

    def __init__(self, nc, ctx, first_mats):
        def sb(name, shape, dt=F32):
            return ctx.enter_context(nc.sbuf_tensor(name, shape, dt))

        self.ones = sb("ones", [P, P])
        self.ident = sb("ident", [P, P])
        self.pick = sb("pick", [P, P], F32R)
        self.mhalf = sb("mhalf", [P, 1])
        self.epst = sb("epst", [P, 1])
        self.epsi = sb("epsi", [P, 1])
        self.v2 = [sb(f"v2{b}", [P, UNITS * GPU, PAIRS, 64]) for b in range(2)]
        self.k4 = [sb(f"k4{b}", [P, GPU, KT, 4, NODES]) for b in range(2)]
        self.raw = [sb(f"raw{m}", [P, KT, D]) for m in range(4)]
        self.s_raw = [nc.alloc_semaphore(f"s_raw{m}") for m in range(4)]
        self.loads = [0] * 4
        c_const = nc.alloc_semaphore("c_const")
        c_zero = nc.alloc_semaphore("c_zero")
        c_pick = nc.alloc_semaphore("c_pick")

        with nc.Block() as block:
            @block.sync
            def _(sp):
                self.load(sp, first_mats)

            @block.gpsimd
            def _(pool):
                nc.gpsimd.memset(self.ones[:, :], 1.0).then_inc(c_const, 1)
                nc.gpsimd.memset(self.mhalf[:, :], -0.5).then_inc(c_const, 1)
                nc.gpsimd.memset(self.epst[:, :], LN_EPS).then_inc(c_const, 1)
                nc.gpsimd.memset(self.epsi[:, :], LN_EPS_INNER).then_inc(c_const, 1)
                pool.wait_ge(c_const, 4)
                nc.gpsimd.affine_select(out=self.ident[:, :], in_=self.ones[:, :], compare_op=ALU.is_equal, fill=0.0,
                                        base=0, pattern=[[-1, P]], channel_multiplier=1).then_inc(c_const, 1)
                for b in range(2):
                    nc.gpsimd.memset(self.k4[b][:, :, :, :, :], 0.0).then_inc(c_zero, 1)

            @block.vector
            def _(dve):
                nc.vector.memset(self.pick[:, :].bitcast(F32), 0.0).then_inc(c_pick, 1)
                dve.wait_ge(c_pick, 1)
                dve.wait_ge(c_const, 4)
                for row in (0, 32):
                    nc.vector.tensor_copy(self.pick[row:row + 1, :], self.ones[row:row + 1, :]).then_inc(c_const, 1)
                for b in range(2):
                    nc.vector.memset(self.v2[b][:, :, :, :], 0.0).then_inc(c_zero, 1)

    def load(self, sp, mats, free=None):
        for m, mat in enumerate(mats):
            if free:
                free(m)
            sp.dma_start(self.raw[m][:, :, :], mat.rearrange("(t p) n -> p t n", p=P)).then_inc(self.s_raw[m], 16)
            self.loads[m] += 1


class Pass:

    def __init__(self, nc, ctx, tag):
        self.nc, self.ctx, self.tag, self.sems = nc, ctx, tag, []

    def sb(self, name, shape, dt=F32):
        return self.ctx.enter_context(self.nc.sbuf_tensor(f"{self.tag}_{name}", shape, dt))

    def ps(self, name, shape):
        return self.ctx.enter_context(self.nc.psum_tensor(f"{self.tag}_{name}", shape, F32))

    def sem(self, name):
        self.sems.append(self.nc.alloc_semaphore(f"{self.tag}_{name}"))
        return self.sems[-1]


def attention_pass(nc, tag, src, dst, adj, weights, scale, transposed, wo, bv, bo, beta, edge_factor, groups,
                   shared, next_mats):
    units = groups * UNITS
    mats, row_bias_cols = weights
    NM = len(mats)
    src_g = src.rearrange("(i u p) d -> i p u d", u=UNITS, p=P)
    adj_g = adj.rearrange("(i u p) k -> i p u k", u=UNITS, p=P)
    src_u = src.rearrange("(i u p) d -> i u p d", u=UNITS, p=P)
    dst_u = dst.rearrange("(i u p) d -> i u p d", u=UNITS, p=P)

    with ExitStack() as ctx:
        a = Pass(nc, ctx, tag)
        W = [a.sb(f"w{m}", [P, 2, KT, D], F32R) for m in range(NM)]
        ident, raw, s_raw = shared.ident, shared.raw, shared.s_raw
        mhalf, epst = shared.mhalf, shared.epst
        loaded = [16 * n for n in shared.loads]
        bvs = a.sb("bvs", [P, PAIRS, 64])
        bos = a.sb("bos", [P, D])
        qkb = a.sb("qkb", [P, 2, KT])
        betas = a.sb("betas", [P, 1])
        xa = a.sb("xa", [P, UNITS, D])
        xT = [a.sb(f"xT{b}", [P, 2, KT, ROWS], F32R) for b in range(2)]
        edge = [a.sb(f"edge{b}", [P, UNITS, NODES]) for b in range(2)]
        off = a.sb("off", [P, UNITS, NODES])
        sbias = [a.sb(f"sbias{b}", [P, UNITS, NODES]) for b in range(2)]
        qT = [a.sb(f"qT{b}", [P, KT, ROWS]) for b in range(2)]
        kT = [a.sb(f"kT{b}", [P, KT, ROWS]) for b in range(2)]
        v2, k4 = shared.v2, shared.k4
        sc = [a.sb(f"sc{b}", [P, HEADS, NODES]) for b in range(2)]
        pr = [a.sb(f"pr{b}", [P, HEADS, NODES]) for b in range(2)]
        st = [a.sb(f"st{b}", [P, 6, HEADS]) for b in range(2)]
        pT = [a.sb(f"pT{b}", [P, PAIRS, P]) for b in range(2)]
        oT = [a.sb(f"oT{b}", [P, 2, KT, P], F32R if wo else F32) for b in range(2)]
        xr = [a.sb(f"xr{b}", [P, D]) for b in range(2)]
        res = [a.sb(f"res{b}", [P, D]) for b in range(2)]
        ln = [a.sb(f"ln{b}", [P, 10]) for b in range(2)]
        yo = [a.sb(f"yo{b}", [P, D]) for b in range(2)]

        ps_s = a.ps("ps_s", [P, 2 * 512])
        ps_t = a.ps("ps_t", [P, 2 * 512])
        ps_o = a.ps("ps_o", [P, 512])
        ps_y = a.ps("ps_y", [P, 512])
        ps_p = [a.ps(f"ps_p{b}", [P, 512]) for b in range(2)]
        ps_w = [*ps_p, ps_o, ps_y]

        s_small = a.sem("s_small")
        c_zero = a.sem("c_zero")
        pe_w, act_w, dve_w = a.sem("pe_w"), a.sem("act_w"), a.sem("dve_w")
        s_xa = a.sem("s_xa")
        s_edge = [a.sem(f"s_edge{b}") for b in range(2)]
        s_xr = [a.sem(f"s_xr{b}") for b in range(2)]
        s_out = [a.sem(f"s_out{b}") for b in range(2)]
        pe_x, pe_p, pe_s, pe_t, pe_o, pe_y = (a.sem(x) for x in ("pe_x", "pe_p", "pe_s", "pe_t", "pe_o", "pe_y"))
        act_x, act_qk, act_v, act_e, act_pT, act_o = (
            a.sem(x) for x in ("act_x", "act_qk", "act_v", "act_e", "act_pT", "act_o"))
        dve_x, dve_off, dve_bias, dve_k4, dve_sc, dve_mx, dve_mn, dve_sum, dve_inv, dve_o = (
            a.sem(x) for x in ("dve_x", "dve_off", "dve_bias", "dve_k4", "dve_sc", "dve_mx", "dve_mn",
                               "dve_sum", "dve_inv", "dve_o"))
        dve_m0, dve_rinv, dve_res, dve_bn, dve_mv, dve_y = (
            a.sem(x) for x in ("dve_m0", "dve_rinv", "dve_res", "dve_bn", "dve_mv", "dve_y"))
        pool_sub, pool_p, pool_ve, pool_rs, pool_v, pool_xr = (
            a.sem(x) for x in ("pool_sub", "pool_p", "pool_ve", "pool_rs", "pool_v", "pool_xr"))

        n_small = 2 + (bo is not None) + (2 if row_bias_cols else 0) + (beta is not None)
        steps = NM * KT
        AHEAD = (("q", 0), ("x", 0), ("q", 1), ("q", 2), ("x", 1), ("k", 0), ("k", 1), ("k", 2), ("x", 2),
                 ("v", 0), ("v", 1), ("v", 2), ("v", 3))
        BETWEEN = (((), (0,), (1, 2)), ((), (3,), (4, 5)), ((6,), (7,), (8, 9)), ((10,), (11,), (12,)))

        def exists(i, pos):
            return inside(i + (2 if AHEAD[pos][0] == "x" else 1), groups)

        def bank_of(par, pos):
            return ps_p[(par + pos) % 2]

        def user_before(i, pos):
            while True:
                pos -= 2
                if pos < 0:
                    i, pos = i - 1, pos + len(AHEAD)
                if exists(i, pos) or isinstance(i, int) and i < -1:
                    return i, AHEAD[pos]

        block = ctx.enter_context(nc.Block())

        @block.sync
        def _(sp):
            sp.dma_start(xa[:, :, :], src_g[0]).then_inc(s_xa, 16)
            sp.wait_ge(c_zero, 1)
            for odd in range(2):
                heads = bv.rearrange("(a h o d) -> a h o d", a=1, o=2, d=32)[:, :, odd, :]
                sp.dma_start(bvs[64 * odd:64 * odd + 64, :, 32 * odd:32 * odd + 32],
                             heads.to_broadcast([64, PAIRS, 32])).then_inc(s_small, 16)
            if bo is not None:
                sp.dma_start(bos[:, :], bo.rearrange("(a d) -> a d", a=1).to_broadcast([P, D])).then_inc(s_small, 16)
            for j, b in enumerate(row_bias_cols or ()):
                sp.dma_start(qkb[:, j, :], b.rearrange("(t p) -> p t", p=P),
                             allow_slow_non_contiguous=True).then_inc(s_small, 16)
            if beta is not None:
                sp.dma_start(betas[:, :], beta.to_broadcast([P, 1])).then_inc(s_small, 16)
            sp.dma_start(edge[0][:, :, :], adj_g[0]).then_inc(s_edge[0], 16)
            sp.wait_ge(pe_x, KT)
            sp.dma_start(xa[:, :, :], src_g[1]).then_inc(s_xa, 16)

            shared.load(sp, next_mats, lambda m: sp.wait_ge(dve_w, KT * min(m + 1, NM)))

            def store(n, i, s):
                if inside(n, units):
                    sp.wait_ge(dve_y, n + 1)
                    sp.dma_start(dst_u[i, s], yo[s % 2][:, :]).then_inc(s_out[s % 2], 16)

            def group(i, pair, par):
                for s in range(UNITS):
                    n = i * UNITS + s
                    if s == 0 and inside(i + 1, groups):
                        if counted((i - 1) * UNITS + UNITS):
                            sp.wait_ge(dve_sc, (i - 1) * UNITS + UNITS)
                        sp.dma_start(edge[1 - par][:, :, :], adj_g[i + 1]).then_inc(s_edge[1 - par], 16)
                    if s == 0 and inside(i + 2, groups):
                        sp.wait_ge(pe_x, KT * (i + 2))
                        sp.dma_start(xa[:, :, :], src_g[i + 2]).then_inc(s_xa, 16)
                    if counted(n - 1):
                        sp.wait_ge(dve_res, n - 1)
                    sp.dma_start(xr[s % 2][:, :], src_u[i, s]).then_inc(s_xr[s % 2], 16)
                    if s >= 2:
                        store(n - 2, i, s - 2)
                    else:
                        store(n - 2, i - 1, s + 2)

            over_groups(sp, groups, group)
            store(units - 2, groups - 1, 2)
            store(units - 1, groups - 1, 3)
            for b in range(2):
                sp.wait_ge(s_out[b], 16 * (units // 2))

        @block.gpsimd
        def _(pool):
            def rstd(n, b):
                if inside(n, units):
                    pool.wait_ge(dve_mv, n + 1)
                    nc.gpsimd.tensor_tensor(ln[b][:, 8:9], ln[b][:, 7:8], epst[:, :], ALU.add).then_inc(pool_ve, 1)
                    pool.wait_ge(pool_ve, n + 1)
                    nc.gpsimd.tensor_tensor(ln[b][:, 9:10], ln[b][:, 8:9], mhalf[:, :], ALU.pow).then_inc(pool_rs, 1)

            def value_bias(n, par, s):
                pool.wait_ge(act_v, n + 1)
                got = v2[par][:, GPU * s:GPU * s + GPU, :, :]
                nc.gpsimd.tensor_tensor(got, got, bvs[:, :, :].unsqueeze(1).to_broadcast([P, GPU, PAIRS, 64]),
                                        ALU.add).then_inc(pool_v, 1)

            def output_bias(n, count, b):
                if not inside(n, units) or bo is None:
                    return
                pool.wait_ge(s_xr[b], 16 * (count + 1))
                nc.gpsimd.tensor_tensor(xr[b][:, :], xr[b][:, :], bos[:, :], ALU.add).then_inc(pool_xr, 1)

            pool.wait_ge(s_small, 16 * n_small)

            def group(i, pair, par):
                for s in range(UNITS):
                    n, b = i * UNITS + s, s % 2
                    rstd(n - 2, b)
                    pool.wait_ge(dve_mx, n + 1)
                    if counted(2 * (n - 1)):
                        pool.wait_ge(pe_t, 2 * (n - 1))
                    nc.gpsimd.tensor_tensor(pr[b][:, :, :], sc[b][:, :, :],
                                            st[b][:, 0, :].unsqueeze(2).to_broadcast([P, HEADS, NODES]),
                                            ALU.subtract).then_inc(pool_sub, 1)
                    value_bias(n, par, s)
                    output_bias(n - 1, pair * 4 + 2 * par + (s - 1) // 2, (s - 1) % 2)
                    pool.wait_ge(dve_rinv, n + 1)
                    nc.gpsimd.tensor_tensor(pr[b][:, :, :], pr[b][:, :, :],
                                            st[b][:, 5, :].unsqueeze(2).to_broadcast([P, HEADS, NODES]),
                                            ALU.mult).then_inc(pool_p, 1)

            over_groups(pool, groups, group)
            output_bias(units - 1, units // 2 - 1, 1)
            rstd(units - 2, 0)
            rstd(units - 1, 1)

        @block.tensor
        def _(pe):
            if transposed:
                for m in range(NM):
                    pe.wait_ge(s_raw[m], loaded[m])
                    for t in range(KT):
                        step = m * KT + t
                        if counted(step - 3):
                            pe.wait_ge(dve_w, step - 3)
                        for o in range(KT):
                            last = nc.tensor.transpose(ps_w[step % 4][:, o * P:(o + 1) * P],
                                                       raw[m][:, o, t * P:(t + 1) * P], ident[:, :])
                        last.then_inc(pe_w, 1)

            def rows_T(g, t, bank):
                for u in range(UNITS):
                    last = nc.tensor.transpose(bank[:, u * P:(u + 1) * P], xa[:, u, t * P:(t + 1) * P], ident[:, :])
                last.then_inc(pe_x, 1)

            def ahead(i, par, pos):
                if not exists(i, pos):
                    return
                bank = bank_of(par, pos)
                at, (kind, o) = user_before(i, pos)
                if kind == "x":
                    if counted(KT * (at + 2) + o + 1):
                        pe.wait_ge(dve_x, KT * (at + 2) + o + 1)
                elif kind == "v":
                    if counted(UNITS * (at + 1) + o + 1):
                        pe.wait_ge(act_v, UNITS * (at + 1) + o + 1)
                else:
                    if counted(6 * (at + 1) + (3 if kind == "k" else 0) + o + 1):
                        pe.wait_ge(act_qk, 6 * (at + 1) + (3 if kind == "k" else 0) + o + 1)
                kind, o = AHEAD[pos]
                if kind == "x":
                    pe.wait_ge(s_xa, 16 * (i + 3))
                    rows_T(i + 2, o, bank)
                    return
                pe.wait_ge(act_x, KT * (i + 2))
                pe.wait_ge(dve_x, KT * (i + 2))
                rows = xT[1 - par]
                if kind == "v":
                    for c, (l, r) in enumerate(SPLIT):
                        for t in range(KT):
                            last = nc.tensor.matmul(bank[:, :D], rows[:, l, t, o * P:(o + 1) * P], W[2][:, r, t, :],
                                                    start=c + t == 0, stop=c == 2 and t == KT - 1)
                else:
                    m = "qk".index(kind)
                    for c, (l, r) in enumerate(SPLIT):
                        for t in range(KT):
                            last = nc.tensor.matmul(bank[:, :], W[m][:, l, t, o * P:(o + 1) * P], rows[:, r, t, :],
                                                    start=c + t == 0, stop=c == 2 and t == KT - 1)
                last.then_inc(pe_p, 1)

            def scores(n, par, s):
                if not inside(n, units):
                    return
                pe.wait_ge(dve_k4, n + 1)
                if counted(n):
                    pe.wait_ge(dve_sc, n)
                for t in range(KT):
                    for g in range(GPU):
                        c = s * P + g * NODES
                        last = nc.tensor.matmul(ps_s[g * NODES:(g + 1) * NODES, t * 256:(t + 1) * 256],
                                                qT[par][:, t, c:c + NODES], k4[s % 2][:, g, t, :, :],
                                                start=True, stop=True)
                last.then_inc(pe_s, 1)

            def probs_T(n, b):
                if not inside(n, units):
                    return
                pe.wait_ge(pool_p, n + 1)
                for h in range(PAIRS):
                    if h in (0, 4):
                        if counted(2 * n - 1 + (h == 4)):
                            pe.wait_ge(act_pT, 2 * n - 1 + (h == 4))
                    last = nc.tensor.transpose(ps_t[:, h * P:(h + 1) * P], pr[b][:, 2 * h:2 * h + 2, :], ident[:, :])
                    if h in (3, 5):
                        last.then_inc(pe_t, 1)

            def values(n, par, s):
                if not inside(n, units):
                    return
                pe.wait_ge(act_pT, 2 * (n + 1))
                pe.wait_ge(pool_v, n + 1)
                if counted(n):
                    pe.wait_ge(act_o, n)
                if wo:
                    if counted(n):
                        pe.wait_ge(dve_o, n)
                for h in range(PAIRS):
                    for g in range(GPU):
                        r = 64 * (h % 2)
                        last = nc.tensor.matmul(ps_o[r:r + 64, (h // 2) * P + g * NODES:(h // 2) * P + (g + 1) * NODES],
                                                v2[par][:, GPU * s + g, h, :], pT[s % 2][:, h, g * NODES:(g + 1) * NODES],
                                                start=True, stop=True)
                last.then_inc(pe_o, 1)

            def output(n, b):
                if not inside(n, units):
                    return
                pe.wait_ge(act_o, n + 1)
                if counted(n):
                    pe.wait_ge(dve_res, n)
                if wo:
                    pe.wait_ge(dve_o, n + 1)
                    for c, (l, r) in enumerate(SPLIT):
                        for t in range(KT):
                            last = nc.tensor.matmul(ps_y[:, :D], oT[b][:, l, t, :], W[3][:, r, t, :],
                                                    start=c + t == 0, stop=c == 2 and t == KT - 1)
                else:
                    for t in range(KT):
                        last = nc.tensor.transpose(ps_y[:, t * P:(t + 1) * P], oT[b][:, 0, t, :], ident[:, :])
                last.then_inc(pe_y, 1)

            pe.wait_ge(s_xa, 16)
            pe.wait_ge(dve_w, steps)
            for t in range(KT):
                if t == 2:
                    pe.wait_ge(dve_x, 1)
                rows_T(0, t, bank_of(1, t - 3))
            for pos in range(len(AHEAD)):
                ahead(-1, 1, pos)

            def fill(i, par, s, c):
                for pos in BETWEEN[s][c]:
                    ahead(i, par, pos)

            def group(i, pair, par):
                for s in range(UNITS):
                    n = i * UNITS + s
                    ppar, ps = (par, s - 1) if s else (1 - par, UNITS - 1)
                    scores(n, par, s)
                    fill(i, par, s, 0)
                    probs_T(n - 1, ps % 2)
                    fill(i, par, s, 1)
                    values(n - 1, ppar, ps)
                    fill(i, par, s, 2)
                    output(n - 1, ps % 2)

            over_groups(pe, groups, group)
            probs_T(units - 1, 1)
            values(units - 1, 1, UNITS - 1)
            output(units - 1, 1)

        @block.scalar
        def _(act):
            for step in range(steps):
                m, t = divmod(step, KT)
                if transposed:
                    act.wait_ge(pe_w, step + 1)
                    nc.scalar.activation(W[m][:, 0, t, :], ps_w[step % 4][:, :D], ACT.Copy).then_inc(act_w, 1)
                else:
                    act.wait_ge(s_raw[m], loaded[m])
                    nc.scalar.activation(W[m][:, 0, t, :], raw[m][:, t, :], ACT.Copy).then_inc(act_w, 1)
            if row_bias_cols:
                act.wait_ge(s_small, 16 * n_small)

            def rows_T(g, gpar, t, bank):
                act.wait_ge(pe_x, KT * g + t + 1)
                nc.scalar.activation(xT[gpar][:, 0, t, :], bank[:, :], ACT.Copy).then_inc(act_x, 1)

            def taken(g, gpar, idx, bank):
                act.wait_ge(pe_p, 10 * g + idx + 1)
                if idx < 6:
                    m, o = divmod(idx, 3)
                    if inside(g - 2, groups):
                        if counted(UNITS * (g - 1)):
                            act.wait_ge(pe_s, UNITS * (g - 1))
                        if counted(UNITS * (g - 1)):
                            act.wait_ge(dve_k4, UNITS * (g - 1))
                    out = (qT, kT)[m][gpar][:, o, :]
                    if row_bias_cols:
                        i = nc.scalar.activation(out, bank[:, :], ACT.Identity, bias=qkb[:, m, o:o + 1])
                    else:
                        i = nc.scalar.activation(out, bank[:, :], ACT.Copy)
                    i.then_inc(act_qk, 1)
                else:
                    u = idx - 6
                    if counted(UNITS * (g - 2) + u + 1):
                        act.wait_ge(pe_o, UNITS * (g - 2) + u + 1)
                    for g2 in range(GPU):
                        for odd in range(2):
                            got = bank[g2 * NODES:(g2 + 1) * NODES, :D].rearrange("p (h o d) -> p h o d", o=2, d=32)
                            i = nc.scalar.activation(v2[gpar][64 * odd:64 * odd + 64, GPU * u + g2, :, 32 * odd:32 * odd + 32],
                                                     got[:, :, odd, :], ACT.Copy)
                    i.then_inc(act_v, 1)

            def ahead(i, par, pos):
                if exists(i, pos):
                    kind, o = AHEAD[pos]
                    if kind == "x":
                        rows_T(i + 2, par, o, bank_of(par, pos))
                    else:
                        taken(i + 1, 1 - par, {"q": 0, "k": 3, "v": 6}[kind] + o, bank_of(par, pos))

            def fill(i, par, s, c):
                for pos in BETWEEN[s][c]:
                    ahead(i, par, pos)

            for t in range(KT):
                rows_T(0, 0, t, bank_of(1, t - 3))
            for pos in range(len(AHEAD)):
                ahead(-1, 1, pos)

            def probs_T(n, b):
                if not inside(n, units):
                    return
                for half, (lo, hi) in enumerate(((0, 4), (4, 6))):
                    act.wait_ge(pe_t, 2 * n + half + 1)
                    if counted(n - 1):
                        act.wait_ge(pe_o, n - 1)
                    nc.scalar.activation(pT[b][:, lo:hi, :], ps_t[:, lo * P:hi * P].rearrange("p (h q) -> p h q", q=P),
                                         ACT.Copy).then_inc(act_pT, 1)

            def exp(n, b):
                act.wait_ge(pool_sub, n + 1)
                nc.scalar.activation(pr[b][:, :, :], pr[b][:, :, :], ACT.Exp).then_inc(act_e, 1)

            def values(n, b):
                if not inside(n, units):
                    return
                act.wait_ge(pe_o, n + 1)
                if counted(n - 1):
                    act.wait_ge(pe_y, n - 1)
                if wo:
                    if counted(n - 1):
                        act.wait_ge(dve_o, n - 1)
                nc.scalar.activation(oT[b][:, 0, :, :], ps_o[:, :D].rearrange("p (t q) -> p t q", q=P),
                                     ACT.Copy).then_inc(act_o, 1)

            def group(i, pair, par):
                for s in range(UNITS):
                    n = i * UNITS + s
                    fill(i, par, s, 0)
                    probs_T(n - 1, (s - 1) % 2)
                    if s < 2:
                        fill(i, par, s, 1)
                        values(n - 1, (s - 1) % 2)
                        exp(n, s % 2)
                    elif s == 2:
                        exp(n, s % 2)
                        fill(i, par, s, 1)
                        values(n - 1, (s - 1) % 2)
                    else:
                        exp(n, s % 2)
                        values(n - 1, (s - 1) % 2)
                        fill(i, par, s, 1)
                    fill(i, par, s, 2)

            over_groups(act, groups, group)
            probs_T(units - 1, 1)
            values(units - 1, 1)

        @block.vector
        def _(dve):
            nc.vector.memset(bvs[:, :, :], 0.0).then_inc(c_zero, 1)
            for step in range(steps):
                m, t = divmod(step, KT)
                dve.wait_ge(act_w, step + 1)
                got = ps_w[step % 4][:, :D] if transposed else raw[m][:, t, :]
                nc.vector.tensor_tensor(W[m][:, 1, t, :], got, W[m][:, 0, t, :].bitcast(F32),
                                        ALU.subtract).then_inc(dve_w, 1)
            def rows_T(g, gpar, t, bank):
                dve.wait_ge(act_x, KT * g + t + 1)
                nc.vector.tensor_tensor(xT[gpar][:, 1, t, :], bank[:, :], xT[gpar][:, 0, t, :].bitcast(F32),
                                        ALU.subtract).then_inc(dve_x, 1)

            def fill(i, par, s):
                for chunk in BETWEEN[s]:
                    for pos in chunk:
                        kind, t = AHEAD[pos]
                        if kind == "x" and exists(i, pos):
                            rows_T(i + 2, par, t, bank_of(par, pos))

            def edges(g, pair, gpar):
                if not inside(g, groups):
                    return
                dve.wait_ge(s_edge[gpar], 16 * (pair + 1))
                if beta is not None:
                    dve.wait_ge(dve_bias, g)
                    nc.vector.tensor_scalar(off[:, :, :], edge[gpar][:, :, :], 0.0, MASKED, ALU.is_le, ALU.mult).then_inc(dve_off, 1)
                    dve.wait_ge(dve_off, g + 1)
                    nc.vector.scalar_tensor_tensor(out=sbias[gpar][:, :, :], in0=edge[gpar][:, :, :], scalar=betas[:, 0:1],
                                                   in1=off[:, :, :], op0=ALU.mult, op1=ALU.add).then_inc(dve_bias, 1)
                else:
                    nc.vector.tensor_scalar(sbias[gpar][:, :, :], edge[gpar][:, :, :], edge_factor, 0.0, ALU.mult, ALU.add).then_inc(dve_bias, 1)

            def spread(n, i, par, s):
                if not inside(n, units):
                    return
                dve.wait_ge(act_qk, 6 * (i + 1))
                if counted(n - 1):
                    dve.wait_ge(pe_s, n - 1)
                for j in range(4):
                    q = slice(32 * j, 32 * j + 32)
                    got = kT[par][q, :, s * P:(s + 1) * P].rearrange("p t (g k) -> p g t k", g=GPU)
                    last = nc.vector.tensor_copy(k4[s % 2][q, :, :, j, :], got)
                last.then_inc(dve_k4, 1)

            def softmax_max(n, par, s):
                b = s % 2
                dve.wait_ge(pe_s, n + 1)
                dve.wait_ge(dve_bias, ni[0] + 1)
                if counted(n - 1):
                    dve.wait_ge(pool_sub, n - 1)
                nc.vector.scalar_tensor_tensor(
                    out=sc[b][:, :, :], in0=ps_s[:, :HEADS * NODES].rearrange("p (h k) -> p h k", k=NODES), scalar=scale,
                    in1=sbias[par][:, s, :].unsqueeze(1).to_broadcast([P, HEADS, NODES]), op0=ALU.mult, op1=ALU.add,
                ).then_inc(dve_sc, 1)
                dve.wait_ge(dve_sc, n + 1)
                if counted(n - 1):
                    dve.wait_ge(pool_p, n - 1)
                nc.vector.tensor_reduce(st[b][:, 0, :], sc[b][:, :, :], AX.X, ALU.max).then_inc(dve_mx, 1)
                if wo:
                    nc.vector.tensor_reduce(st[b][:, 1, :], sc[b][:, :, :], AX.X, ALU.min).then_inc(dve_mn, 1)

            def softmax_sum(n, s):
                b = s % 2
                dve.wait_ge(act_e, n + 1)
                nc.vector.tensor_reduce(st[b][:, 2, :], pr[b][:, :, :], AX.X, ALU.add).then_inc(dve_sum, 1)
                if wo:
                    dve.wait_ge(dve_mn, n + 1)
                    dve.wait_ge(dve_mx, n + 1)
                    nc.vector.scalar_tensor_tensor(out=st[b][:, 3, :], in0=st[b][:, 1, :], scalar=-1.0, in1=st[b][:, 0, :],
                                                   op0=ALU.mult, op1=ALU.max).then_inc(dve_m0, 1)
                    dve.wait_ge(dve_sum, n + 1)
                    nc.vector.reciprocal(st[b][:, 4, :], st[b][:, 2, :]).then_inc(dve_inv, 1)
                    dve.wait_ge(dve_inv, n + 1)
                    dve.wait_ge(dve_m0, n + 1)
                    nc.vector.scalar_tensor_tensor(out=st[b][:, 5, :], in0=st[b][:, 3, :], scalar=0.0, in1=st[b][:, 4, :],
                                                   op0=ALU.not_equal, op1=ALU.mult).then_inc(dve_rinv, 1)
                else:
                    dve.wait_ge(dve_sum, n + 1)
                    nc.vector.reciprocal(st[b][:, 5, :], st[b][:, 2, :]).then_inc(dve_rinv, 1)

            def low_part(n, b):
                if not inside(n, units) or not wo:
                    return
                dve.wait_ge(act_o, n + 1)
                nc.vector.tensor_tensor(oT[b][:, 1, :, :], ps_o[:, :D].rearrange("p (t q) -> p t q", q=P),
                                        oT[b][:, 0, :, :].bitcast(F32), ALU.subtract).then_inc(dve_o, 1)

            def residual(n, count, b):
                if not inside(n, units):
                    return
                dve.wait_ge(pe_y, n + 1)
                if bo is None:
                    dve.wait_ge(s_xr[b], 16 * (count + 1))
                else:
                    dve.wait_ge(pool_xr, n + 1)
                nc.vector.tensor_tensor(res[b][:, :], ps_y[:, :D], xr[b][:, :], ALU.add).then_inc(dve_res, 1)
                dve.wait_ge(dve_res, n + 1)
                nc.vector.bn_stats(ln[b][:, 0:6], res[b][:, :]).then_inc(dve_bn, 1)
                dve.wait_ge(s_small, 16)
                dve.wait_ge(dve_bn, n + 1)
                nc.vector.bn_aggr(ln[b][:, 6:8], ln[b][:, 0:6]).then_inc(dve_mv, 1)

            def normed(n, count, b):
                if not inside(n, units):
                    return
                dve.wait_ge(pool_rs, n + 1)
                dve.wait_ge(dve_mv, n + 1)
                if counted(16 * count):
                    dve.wait_ge(s_out[b], 16 * count)
                nc.vector.tensor_scalar(yo[b][:, :], res[b][:, :], ln[b][:, 6:7], ln[b][:, 9:10], ALU.subtract,
                                        ALU.mult).then_inc(dve_y, 1)

            if row_bias_cols or beta is not None:
                dve.wait_ge(s_small, 16 * n_small)
            for t in range(KT):
                rows_T(0, 0, t, bank_of(1, t - 3))
            edges(0, 0, 0)
            fill(-1, 1, 0)
            fill(-1, 1, 1)
            fill(-1, 1, 2)
            spread(0, 0, 0, 0)
            fill(-1, 1, 3)
            ni = [0]

            def group(i, pair, par):
                ni[0] = i
                for s in range(UNITS):
                    n = i * UNITS + s
                    count = pair * 4 + 2 * par + s // 2 - 1
                    residual(n - 2, count, s % 2)
                    softmax_max(n, par, s)
                    normed(n - 2, count, s % 2)
                    if s < UNITS - 1:
                        spread(n + 1, i, par, s + 1)
                    else:
                        spread(n + 1, i + 1, 1 - par, 0)
                    if s == 2:
                        edges(i + 1, pair + (1 if par else 0), 1 - par)
                    low_part(n - 1, (s - 1) % 2)
                    softmax_sum(n, s)
                    fill(i, par, s)

            over_groups(dve, groups, group)
            low_part(units - 1, 1)
            for n in (units - 2, units - 1):
                residual(n, n // 2, n % 2)
                normed(n, n // 2, n % 2)

    nc.clear_and_free_semaphores(a.sems)
    nc.all_engine_barrier()


def digcn_pass(nc, tag, src, dst, adj, mats, row_biases, ln_scale, ln_shift, residual_src, groups, shared,
               next_mats):
    units = groups * UNITS
    LEFT, RIGHT, SELF = range(3)
    src_g = src.rearrange("(i u p) d -> i p u d", u=UNITS, p=P)
    adj_g = adj.rearrange("(i u p) k -> i p u k", u=UNITS, p=P)
    dst_u = dst.rearrange("(i u p) d -> i u p d", u=UNITS, p=P)
    ends = residual_src is not None
    if ends:
        res_u = residual_src.rearrange("(i u p) d -> i u p d", u=UNITS, p=P)

    with ExitStack() as ctx:
        a = Pass(nc, ctx, tag)
        W = [a.sb(f"w{m}", [P, 2, KT, D], F32R) for m in range(3)]
        ident, ones, pick, raw, s_raw = shared.ident, shared.ones, shared.pick, shared.raw, shared.s_raw
        mhalf, epst, epsi = shared.mhalf, shared.epst, shared.epsi
        loaded = [16 * n for n in shared.loads]
        brow = a.sb("brow", [P, 3, D])
        bround = a.sb("bround", [P, 3, D], F32R)
        bias = a.sb("bias", [P, 3, D], F32R)
        gain = a.sb("gain", [P, D])
        shift = a.sb("shift", [P, D])
        after = a.sb("after", [P, P])
        before = a.sb("before", [P, P])
        same = a.sb("same", [P, NODES])
        xa = a.sb("xa", [P, UNITS, D])
        hT = [a.sb(f"hT{b}", [P, 2, KT, ROWS], F32R) for b in range(2)]
        edge = [a.sb(f"edge{b}", [P, UNITS, NODES]) for b in range(2)]
        half = a.sb("half", [P, UNITS, NODES])
        u0 = a.sb("u0", [P, UNITS, NODES])
        u1 = a.sb("u1", [P, UNITS, NODES])
        u2 = a.sb("u2", [P, UNITS, NODES])
        u3 = a.sb("u3", [P, UNITS, NODES])
        u4 = a.sb("u4", [P, UNITS, NODES])
        u5 = a.sb("u5", [P, UNITS, NODES])
        u6 = a.sb("u6", [P, UNITS, NODES])
        st = a.sb("st", [P, 6, UNITS])
        diag = [a.sb(f"diag{b}", [P, UNITS]) for b in range(2)]
        wide = a.sb("wide", [P, UNITS, P])
        part = [a.sb(f"part{m}", [P, UNITS, P]) for m in range(2)]
        aT = [a.sb(f"aT{b}", [P, 2, 2, UNITS, P], F32R) for b in range(2)]
        hp = [a.sb(f"hp{b}", [P, 2, 2, D], F32R) for b in range(2)]
        hs = [a.sb(f"hs{b}", [P, D]) for b in range(2)]
        c0 = [a.sb(f"c0{b}", [P, D]) for b in range(2)]
        c1 = [a.sb(f"c1{b}", [P, D]) for b in range(2)]
        c2 = [a.sb(f"c2{b}", [P, D]) for b in range(2)]
        ln = [a.sb(f"ln{b}", [P, 20]) for b in range(2)]
        xr = [a.sb(f"xr{b}", [P, D]) for b in range(2)]
        c3 = [a.sb(f"c3{b}", [P, D]) for b in range(2)]
        yo = [a.sb(f"yo{b}", [P, D]) for b in range(2)]

        ps_h = [a.ps(f"ps_h{m}", [P, 512]) for m in range(3)]
        ps_c = a.ps("ps_c", [P, 512])
        ps_u = a.ps("ps_u", [P, 2 * 512])
        ps_a = a.ps("ps_a", [P, 512])
        ps_x = a.ps("ps_x", [P, 512])
        ps_w = [*ps_h, ps_c]

        s_edge = [a.sem(f"s_edge{b}") for b in range(2)]
        s_xr = [a.sem(f"s_xr{b}") for b in range(2)]
        s_out = [a.sem(f"s_out{b}") for b in range(2)]
        s_small, s_xa, c_zero, c_row, c_mask = (a.sem(x) for x in ("s_small", "s_xa", "c_zero", "c_row", "c_mask"))
        pe_w, act_w, dve_w = a.sem("pe_w"), a.sem("act_w"), a.sem("dve_w")
        pe_x, pe_h, pe_u, pe_a, pe_c = (a.sem(x) for x in ("pe_x", "pe_h", "pe_u", "pe_a", "pe_c"))
        act_x, act_h, act_half, act_e, act_a, act_y = (
            a.sem(x) for x in ("act_x", "act_h", "act_half", "act_e", "act_a", "act_y"))
        dve_x, dve_h, dve_u, dve_mx, dve_sum, dve_inv, dve_dsum, dve_deps, dve_rs, dve_attn, dve_wide, dve_dg, dve_part = (
            a.sem(x) for x in ("dve_x", "dve_h", "dve_u", "dve_mx", "dve_sum", "dve_inv", "dve_dsum", "dve_deps",
                               "dve_rs", "dve_attn", "dve_wide", "dve_dg", "dve_part"))
        dve_c, dve_bn, dve_mv, dve_g, dve_o, dve_r, dve_bn2, dve_mv2, dve_y = (
            a.sem(x) for x in ("dve_c", "dve_bn", "dve_mv", "dve_g", "dve_o", "dve_r", "dve_bn2", "dve_mv2", "dve_y"))
        pool_sub, pool_p, pool_d, pool_pick, pool_a, pool_ve, pool_rs, pool_ve2, pool_rs2 = (
            a.sem(x) for x in ("pool_sub", "pool_p", "pool_d", "pool_pick", "pool_a", "pool_ve", "pool_rs", "pool_ve2", "pool_rs2"))

        n_small = 3 * 2 + 2
        steps = 3 * KT
        zeros = 2
        masks = 3
        rows_ready = 3 * 2
        items = {LEFT: 0, RIGHT: 1, SELF: 2}

        block = ctx.enter_context(nc.Block())

        @block.sync
        def _(sp):
            sp.dma_start(xa[:, :, :], src_g[0]).then_inc(s_xa, 16)
            sp.dma_start(edge[0][:, :, :], adj_g[0]).then_inc(s_edge[0], 16)
            for j, b in enumerate(row_biases):
                for row in (0, 32):
                    sp.dma_start(brow[row:row + 1, j, :], b).then_inc(s_small, 16)
            sp.dma_start(gain[:, :], ln_scale.to_broadcast([P, D])).then_inc(s_small, 16)
            sp.dma_start(shift[:, :], ln_shift.to_broadcast([P, D])).then_inc(s_small, 16)
            sp.wait_ge(pe_x, KT)
            sp.dma_start(xa[:, :, :], src_g[1]).then_inc(s_xa, 16)

            shared.load(sp, next_mats, lambda m: sp.wait_ge(dve_w, KT * min(m + 1, 3)))

            def store(n, i, s):
                if inside(n, units):
                    sp.wait_ge(dve_y if ends else act_y, n + 1)
                    sp.dma_start(dst_u[i, s], yo[s % 2][:, :]).then_inc(s_out[s % 2], 16)

            def group(i, pair, par):
                for s in range(UNITS):
                    n = i * UNITS + s
                    if s == 1 and inside(i + 1, groups):
                        if counted(i):
                            sp.wait_ge(pool_d, i)
                        sp.dma_start(edge[1 - par][:, :, :], adj_g[i + 1]).then_inc(s_edge[1 - par], 16)
                    if s == 1 and inside(i + 2, groups):
                        sp.wait_ge(pe_x, KT * (i + 2))
                        sp.dma_start(xa[:, :, :], src_g[i + 2]).then_inc(s_xa, 16)
                    if ends:
                        if counted(n - 1):
                            sp.wait_ge(dve_r, n - 1)
                        sp.dma_start(xr[s % 2][:, :], res_u[i, s]).then_inc(s_xr[s % 2], 16)
                    if s >= 2:
                        store(n - 2, i, s - 2)
                    else:
                        store(n - 2, i - 1, s + 2)

            over_groups(sp, groups, group)
            store(units - 2, groups - 1, 2)
            store(units - 1, groups - 1, 3)
            for b in range(2):
                sp.wait_ge(s_out[b], 16 * (units // 2))

        @block.gpsimd
        def _(pool):
            nc.gpsimd.affine_select(out=after[:, :], in_=ones[:, :], compare_op=ALU.is_gt, fill=0.0,
                                    base=0, pattern=[[-1, P]], channel_multiplier=1).then_inc(c_mask, 1)
            nc.gpsimd.affine_select(out=before[:, :], in_=ones[:, :], compare_op=ALU.is_gt, fill=0.0,
                                    base=0, pattern=[[1, P]], channel_multiplier=-1).then_inc(c_mask, 1)
            nc.gpsimd.tensor_tensor(same[:, :], ident[:, 0:NODES], ident[:, NODES:P], ALU.add).then_inc(c_mask, 1)

            def attention(g, gpar, step):
                if not inside(g, groups):
                    return
                if step == 0:
                    pool.wait_ge(dve_mx, g + 1)
                    nc.gpsimd.tensor_tensor(u1[:, :, :], u0[:, :, :], st[:, 0, :].unsqueeze(2).to_broadcast([P, UNITS, NODES]),
                                            ALU.subtract).then_inc(pool_sub, 1)
                elif step == 1:
                    pool.wait_ge(dve_inv, g + 1)
                    nc.gpsimd.tensor_tensor(u3[:, :, :], u2[:, :, :], st[:, 2, :].unsqueeze(2).to_broadcast([P, UNITS, NODES]),
                                            ALU.mult).then_inc(pool_p, 1)
                    pool.wait_ge(pool_p, g + 1)
                    pool.wait_ge(s_edge[gpar], 16 * (gpair(g, gpar) + 1))
                    nc.gpsimd.tensor_tensor(u4[:, :, :], u3[:, :, :], edge[gpar][:, :, :], ALU.mult).then_inc(pool_d, 1)
                elif step == 2:
                    pool.wait_ge(dve_attn, g + 1)
                    pool.wait_ge(c_mask, masks)
                    nc.gpsimd.tensor_tensor(u6[:, :, :], u5[:, :, :], same[:, :].unsqueeze(1).to_broadcast([P, UNITS, NODES]),
                                            ALU.mult).then_inc(pool_pick, 1)
                else:
                    for m in range(2):
                        pool.wait_ge(act_a, 2 * g + m + 1)
                        nc.gpsimd.tensor_tensor(aT[gpar][:, m, 1, :, :], part[m][:, :, :],
                                                aT[gpar][:, m, 0, :, :].bitcast(F32), ALU.subtract).then_inc(pool_a, 1)

            def gpair(g, gpar):
                return g // 2 if isinstance(g, int) else pi[0] + (1 if gpar == 0 else 0)

            pi = [0]

            def rstd(n, b, eps, at, ready, ve, rs):
                if inside(n, units):
                    pool.wait_ge(ready, n + 1)
                    nc.gpsimd.tensor_tensor(ln[b][:, at + 2:at + 3], ln[b][:, at + 1:at + 2], eps[:, :], ALU.add).then_inc(ve, 1)
                    pool.wait_ge(ve, n + 1)
                    nc.gpsimd.tensor_tensor(ln[b][:, at + 3:at + 4], ln[b][:, at + 2:at + 3], mhalf[:, :], ALU.pow).then_inc(rs, 1)

            for step in range(4):
                attention(0, 0, step)

            def group(i, pair, par):
                pi[0] = pair
                for s in range(UNITS):
                    n = i * UNITS + s
                    if ends:
                        rstd(n - 2, s % 2, epst, 16, dve_mv2, pool_ve2, pool_rs2)
                    rstd(n - 1, (s - 1) % 2, epsi, 6, dve_mv, pool_ve, pool_rs)
                    for step in ((), (0,), (1, 2), (3,))[s]:
                        attention(i + 1, 1 - par, step)

            over_groups(pool, groups, group)
            rstd(units - 1, 1, epsi, 6, dve_mv, pool_ve, pool_rs)
            if ends:
                rstd(units - 2, 0, epst, 16, dve_mv2, pool_ve2, pool_rs2)
                rstd(units - 1, 1, epst, 16, dve_mv2, pool_ve2, pool_rs2)

        @block.tensor
        def _(pe):
            for m in range(3):
                pe.wait_ge(s_raw[m], loaded[m])
                for t in range(KT):
                    step = m * KT + t
                    if counted(step - 3):
                        pe.wait_ge(dve_w, step - 3)
                    for o in range(KT):
                        last = nc.tensor.transpose(ps_w[step % 4][:, o * P:(o + 1) * P],
                                                   raw[m][:, o, t * P:(t + 1) * P], ident[:, :])
                    last.then_inc(pe_w, 1)

            def rows_T(g, tiles=range(KT)):
                if not inside(g, groups):
                    return
                pe.wait_ge(s_xa, 16 * (g + 1))
                for t in tiles:
                    if counted(KT * g + t):
                        pe.wait_ge(dve_x, KT * g + t)
                    for u in range(UNITS):
                        last = nc.tensor.transpose(ps_x[:, u * P:(u + 1) * P], xa[:, u, t * P:(t + 1) * P], ident[:, :])
                    last.then_inc(pe_x, 1)

            def products(g, gpar):
                if not inside(g, groups):
                    return
                pe.wait_ge(act_x, KT * (g + 1))
                pe.wait_ge(dve_x, KT * (g + 1))
                if counted(2 * g):
                    pe.wait_ge(dve_u, 2 * g)
                for u in range(UNITS):
                    q = slice(u * P, (u + 1) * P)
                    for c in range(2):
                        for t in range(KT):
                            last = nc.tensor.matmul(ps_u[:, u * 256:(u + 1) * 256], hT[gpar][:, c, t, q],
                                                    hT[gpar][:, :, t, q], start=c + t == 0, stop=c == 1 and t == KT - 1)
                last.then_inc(pe_u, 1)

            def attention_T(g):
                if not inside(g, groups):
                    return
                pe.wait_ge(dve_wide, 2 * (g + 1))
                if counted(2 * g):
                    pe.wait_ge(dve_part, 2 * g)
                for u in range(UNITS):
                    last = nc.tensor.transpose(ps_a[:, u * P:(u + 1) * P], wide[:, u, :], ident[:, :])
                last.then_inc(pe_a, 1)

            def project(n, gpar, s, m):
                if m == SELF:
                    if counted(3 * n):
                        pe.wait_ge(act_h, 3 * n)
                else:
                    if counted(2 * (n - 1) + m + 1):
                        pe.wait_ge(dve_h, 2 * (n - 1) + m + 1)
                for c, (l, r) in enumerate(SPLIT):
                    for t in range(KT):
                        nc.tensor.matmul(ps_h[m][:, :D], hT[gpar][:, l, t, s * P:(s + 1) * P], W[m][:, r, t, :],
                                         start=c + t == 0, stop=False)
                nc.tensor.matmul(ps_h[m][:, :D], pick[:, :], bias[:, m, :], start=False, stop=True).then_inc(pe_h, 1)

            def context(n, gpar, s):
                if not inside(n, units):
                    return
                if counted(3 * (n + 1) - 1):
                    pe.wait_ge(act_h, 3 * (n + 1) - 1)
                pe.wait_ge(dve_h, 2 * (n + 1))
                if counted(ga[0]):
                    pe.wait_ge(pool_a, ga[0])
                if counted(n):
                    pe.wait_ge(dve_c, n)
                for m in range(2):
                    for c, (l, r) in enumerate(SPLIT):
                        last = nc.tensor.matmul(ps_c[:, :D], aT[gpar][:, m, l, s, :], hp[s % 2][:, m, r, :],
                                                start=m + c == 0, stop=m == 1 and c == 2)
                last.then_inc(pe_c, 1)

            ga = [0]
            pe.wait_ge(act_w, steps)
            pe.wait_ge(dve_w, steps)
            rows_T(0)
            products(0, 0)
            pe.wait_ge(c_zero, zeros)
            attention_T(0)
            pe.wait_ge(c_row, rows_ready)

            def group(i, pair, par):
                for s in range(UNITS):
                    n = i * UNITS + s
                    if s:
                        ppar, ps, ga[0] = par, s - 1, 2 * (i + 1)
                    else:
                        ppar, ps, ga[0] = 1 - par, UNITS - 1, 2 * i
                    project(n, par, s, LEFT)
                    if s < 2:
                        rows_T(i + 1, (2 * s,))
                    context(n - 1, ppar, ps)
                    project(n, par, s, RIGHT)
                    if s == 3:
                        attention_T(i + 1)
                    if s == 0:
                        rows_T(i + 1, (1,))
                    if s == 1:
                        products(i + 1, 1 - par)
                    project(n, par, s, SELF)

            over_groups(pe, groups, group)
            ga[0] = 2 * groups
            context(units - 1, 1, UNITS - 1)

        @block.scalar
        def _(act):
            for step in range(steps):
                m, t = divmod(step, KT)
                act.wait_ge(pe_w, step + 1)
                nc.scalar.activation(W[m][:, 0, t, :], ps_w[step % 4][:, :D], ACT.Copy).then_inc(act_w, 1)
            act.wait_ge(s_small, 16 * n_small)
            act.wait_ge(c_zero, zeros)
            for j in range(3):
                nc.scalar.activation(bias[0:1, j, :], brow[0:1, j, :], ACT.Copy).then_inc(c_row, 1)
                nc.scalar.activation(bround[32:33, j, :], brow[32:33, j, :], ACT.Copy).then_inc(act_w, 1)

            def rows_T(g, gpar, tiles=range(KT)):
                if not inside(g, groups):
                    return
                for t in tiles:
                    act.wait_ge(pe_x, KT * g + t + 1)
                    nc.scalar.activation(hT[gpar][:, 0, t, :], ps_x[:, :], ACT.Copy).then_inc(act_x, 1)

            def attention(g, gpar, step):
                if not inside(g, groups):
                    return
                if step == 0:
                    act.wait_ge(pe_u, g + 1)
                    if counted(2 * g):
                        act.wait_ge(dve_u, 2 * g)
                    for b in range(GPU):
                        q = slice(b * NODES, (b + 1) * NODES)
                        nc.scalar.activation(half[q, :, :], ps_u[q, :].rearrange("p (u c) -> p u c", u=UNITS)[
                            :, :, P + b * NODES:P + (b + 1) * NODES], ACT.Copy).then_inc(act_half, 1)
                elif step == 1:
                    act.wait_ge(pool_sub, g + 1)
                    nc.scalar.activation(u2[:, :, :], u1[:, :, :], ACT.Exp, scale=float(D) ** -0.5).then_inc(act_e, 1)
                else:
                    for m in range(2):
                        act.wait_ge(dve_part, 2 * g + m + 1)
                        nc.scalar.activation(aT[gpar][:, m, 0, :, :], part[m][:, :, :], ACT.Copy).then_inc(act_a, 1)

            def left_right(n, b, m):
                act.wait_ge(pe_h, 3 * n + m + 1)
                if counted(n - 1):
                    act.wait_ge(pe_c, n - 1)
                nc.scalar.activation(hp[b][:, m, 0, :], ps_h[m][:, :D], ACT.Copy).then_inc(act_h, 1)

            def relu(n, count, b):
                if inside(n, units) and not ends:
                    act.wait_ge(dve_o, n + 1)
                    if counted(16 * count):
                        act.wait_ge(s_out[b], 16 * count)
                    nc.scalar.activation(yo[b][:, :], c2[b][:, :], ACT.Relu).then_inc(act_y, 1)

            rows_T(0, 0)
            for step in range(3):
                attention(0, 0, step)

            def group(i, pair, par):
                for s in range(UNITS):
                    n, b = i * UNITS + s, s % 2
                    left_right(n, b, LEFT)
                    if s < 2:
                        rows_T(i + 1, 1 - par, (2 * s,))
                    if s == 2:
                        attention(i + 1, 1 - par, 1)
                    left_right(n, b, RIGHT)
                    if s == 0:
                        rows_T(i + 1, 1 - par, (1,))
                    relu(n - 2, pair * 4 + 2 * par + s // 2 - 1, b)
                    act.wait_ge(pe_h, 3 * n + 3)
                    act.wait_ge(dve_dg, i + 1)
                    if counted(n - 1):
                        act.wait_ge(dve_c, n - 1)
                    nc.scalar.activation(hs[b][:, :], ps_h[SELF][:, :D], ACT.Copy, scale=diag[par][:, s:s + 1]).then_inc(act_h, 1)
                    if s == 1:
                        attention(i + 1, 1 - par, 0)
                    if s == 3:
                        attention(i + 1, 1 - par, 2)

            over_groups(act, groups, group)
            relu(units - 2, units // 2 - 1, 0)
            relu(units - 1, units // 2 - 1, 1)

        @block.vector
        def _(dve):
            nc.vector.memset(bias[:, :, :].bitcast(F32), 0.0).then_inc(c_zero, 1)
            nc.vector.memset(wide[:, :, :], 0.0).then_inc(c_zero, 1)
            for step in range(steps):
                m, t = divmod(step, KT)
                dve.wait_ge(act_w, step + 1)
                nc.vector.tensor_tensor(W[m][:, 1, t, :], ps_w[step % 4][:, :D], W[m][:, 0, t, :].bitcast(F32),
                                        ALU.subtract).then_inc(dve_w, 1)
            dve.wait_ge(act_w, steps + 3)
            dve.wait_ge(s_small, 16 * n_small)
            for j in range(3):
                nc.vector.tensor_tensor(bias[32:33, j, :], brow[32:33, j, :], bround[32:33, j, :].bitcast(F32),
                                        ALU.subtract).then_inc(c_row, 1)
            dve.wait_ge(c_mask, masks)

            def rows_T(g, gpar, tiles=range(KT)):
                if not inside(g, groups):
                    return
                for t in tiles:
                    dve.wait_ge(act_x, KT * g + t + 1)
                    nc.vector.tensor_tensor(hT[gpar][:, 1, t, :], ps_x[:, :], hT[gpar][:, 0, t, :].bitcast(F32),
                                            ALU.subtract).then_inc(dve_x, 1)

            def attention(g, gpar, step):
                if not inside(g, groups):
                    return
                if step == 0:
                    dve.wait_ge(act_half, 2 * (g + 1))
                    dve.wait_ge(pool_sub, g)
                    for b in range(GPU):
                        q = slice(b * NODES, (b + 1) * NODES)
                        nc.vector.tensor_tensor(u0[q, :, :], ps_u[q, :].rearrange("p (u c) -> p u c", u=UNITS)[
                            :, :, b * NODES:(b + 1) * NODES], half[q, :, :], ALU.add).then_inc(dve_u, 1)
                    dve.wait_ge(dve_u, 2 * (g + 1))
                    nc.vector.tensor_reduce(st[:, 0, :], u0[:, :, :], AX.X, ALU.max).then_inc(dve_mx, 1)
                elif step == 1:
                    dve.wait_ge(act_e, g + 1)
                    nc.vector.tensor_reduce(st[:, 1, :], u2[:, :, :], AX.X, ALU.add).then_inc(dve_sum, 1)
                    dve.wait_ge(dve_sum, g + 1)
                    nc.vector.reciprocal(st[:, 2, :], st[:, 1, :]).then_inc(dve_inv, 1)
                elif step == 2:
                    dve.wait_ge(pool_d, g + 1)
                    nc.vector.tensor_reduce(st[:, 3, :], u4[:, :, :], AX.X, ALU.add).then_inc(dve_dsum, 1)
                    dve.wait_ge(dve_dsum, g + 1)
                    nc.vector.tensor_scalar(st[:, 4, :], st[:, 3, :], 1e-10, 0.0, ALU.add, ALU.add).then_inc(dve_deps, 1)
                    dve.wait_ge(dve_deps, g + 1)
                    nc.vector.reciprocal(st[:, 5, :], st[:, 4, :]).then_inc(dve_rs, 1)
                    dve.wait_ge(dve_rs, g + 1)
                    dve.wait_ge(pe_a, g)
                    dve.wait_ge(pool_pick, g)
                    nc.vector.tensor_tensor(u5[:, :, :], u4[:, :, :], st[:, 5, :].unsqueeze(2).to_broadcast([P, UNITS, NODES]),
                                            ALU.mult).then_inc(dve_attn, 1)
                    dve.wait_ge(dve_attn, g + 1)
                    for b in range(GPU):
                        q = slice(b * NODES, (b + 1) * NODES)
                        nc.vector.tensor_copy(wide[q, :, b * NODES:(b + 1) * NODES], u5[q, :, :]).then_inc(dve_wide, 1)
                elif step == 3:
                    dve.wait_ge(pool_pick, g + 1)
                    nc.vector.tensor_reduce(diag[gpar][:, :], u6[:, :, :], AX.X, ALU.add).then_inc(dve_dg, 1)
                else:
                    dve.wait_ge(pe_a, g + 1)
                    if counted(2 * g):
                        dve.wait_ge(pool_a, 2 * g)
                    for m, mask in enumerate((after, before)):
                        nc.vector.tensor_tensor(part[m][:, :, :], ps_a[:, :].rearrange("p (u q) -> p u q", u=UNITS),
                                                mask[:, :].unsqueeze(1).to_broadcast([P, UNITS, P]), ALU.mult).then_inc(dve_part, 1)

            def left_right(n, b, m):
                dve.wait_ge(act_h, 3 * n + m + 1)
                nc.vector.tensor_tensor(hp[b][:, m, 1, :], ps_h[m][:, :D], hp[b][:, m, 0, :].bitcast(F32),
                                        ALU.subtract).then_inc(dve_h, 1)

            def context(n, b):
                if not inside(n, units):
                    return
                dve.wait_ge(pe_c, n + 1)
                dve.wait_ge(act_h, 3 * (n + 1))
                nc.vector.tensor_tensor(c0[b][:, :], ps_c[:, :D], hs[b][:, :], ALU.add).then_inc(dve_c, 1)
                dve.wait_ge(dve_c, n + 1)
                nc.vector.bn_stats(ln[b][:, 0:6], c0[b][:, :]).then_inc(dve_bn, 1)
                dve.wait_ge(c_zero, 1)
                dve.wait_ge(dve_bn, n + 1)
                nc.vector.bn_aggr(ln[b][:, 6:8], ln[b][:, 0:6]).then_inc(dve_mv, 1)

            def inner_norm(n, count, b):
                if not inside(n, units):
                    return
                dve.wait_ge(dve_mv, n + 1)
                nc.vector.scalar_tensor_tensor(out=c1[b][:, :], in0=c0[b][:, :], scalar=ln[b][:, 6:7], in1=gain[:, :],
                                               op0=ALU.subtract, op1=ALU.mult).then_inc(dve_g, 1)
                dve.wait_ge(dve_g, n + 1)
                dve.wait_ge(pool_rs, n + 1)
                if not ends:
                    if counted(n - 1):
                        dve.wait_ge(act_y, n - 1)
                nc.vector.scalar_tensor_tensor(out=c2[b][:, :], in0=c1[b][:, :], scalar=ln[b][:, 9:10], in1=shift[:, :],
                                               op0=ALU.mult, op1=ALU.add).then_inc(dve_o, 1)
                if ends:
                    dve.wait_ge(dve_o, n + 1)
                    dve.wait_ge(s_xr[b], 16 * (count + 1))
                    nc.vector.scalar_tensor_tensor(out=c3[b][:, :], in0=c2[b][:, :], scalar=0.0, in1=xr[b][:, :],
                                                   op0=ALU.max, op1=ALU.add).then_inc(dve_r, 1)
                    dve.wait_ge(dve_r, n + 1)
                    nc.vector.bn_stats(ln[b][:, 10:16], c3[b][:, :]).then_inc(dve_bn2, 1)
                    dve.wait_ge(c_zero, 1)
                    dve.wait_ge(dve_bn2, n + 1)
                    nc.vector.bn_aggr(ln[b][:, 16:18], ln[b][:, 10:16]).then_inc(dve_mv2, 1)

            def normed(n, count, b):
                if not inside(n, units) or not ends:
                    return
                dve.wait_ge(pool_rs2, n + 1)
                if counted(16 * count):
                    dve.wait_ge(s_out[b], 16 * count)
                nc.vector.tensor_scalar(yo[b][:, :], c3[b][:, :], ln[b][:, 16:17], ln[b][:, 19:20], ALU.subtract,
                                        ALU.mult).then_inc(dve_y, 1)

            rows_T(0, 0)
            for step in range(5):
                attention(0, 0, step)

            def group(i, pair, par):
                for s in range(UNITS):
                    n, b = i * UNITS + s, s % 2
                    left_right(n, b, LEFT)
                    if s < 2:
                        rows_T(i + 1, 1 - par, (2 * s,))
                    context(n - 1, 1 - b)
                    if s == 2:
                        attention(i + 1, 1 - par, 1)
                    left_right(n, b, RIGHT)
                    if s == 3:
                        attention(i + 1, 1 - par, 3)
                        attention(i + 1, 1 - par, 4)
                    if s == 0:
                        rows_T(i + 1, 1 - par, (1,))
                    normed(n - 2, pair * 4 + 2 * par + s // 2 - 1, b)
                    inner_norm(n - 1, pair * 4 + 2 * par + (s + 1) // 2 - 1, 1 - b)
                    if s == 1:
                        attention(i + 1, 1 - par, 0)
                    if s == 2:
                        attention(i + 1, 1 - par, 2)

            over_groups(dve, groups, group)
            context(units - 1, 1)
            normed(units - 2, units // 2 - 1, 0)
            inner_norm(units - 1, units // 2 - 1, 1)
            normed(units - 1, units // 2 - 1, 1)

    nc.clear_and_free_semaphores(a.sems)
    nc.all_engine_barrier()


def graph_layers(nc, ins, out):
    def flat(name):
        return ins[name].rearrange("b n d -> (b n) d")

    x, adj = flat("x"), flat("adj")
    groups = x.shape[0] // ROWS
    kept = [nc.dram_tensor(f"rows{k}", (x.shape[0], D), F32, kind="Internal").ap() for k in range(4)]
    y = out.rearrange("b n d -> (b n) d")
    l0, l1, l2, l3 = (lambda k, layer=layer: ins[f"L{layer}_gnn_{k}"] for layer in range(4))

    w0 = [l0(k) for k in ("Wq", "Wk", "Wv", "Wo")]
    w1 = [l1(k) for k in ("Wq", "Wk", "Wv")]
    w2 = [[l2(m)[k] for m in ("Wl", "Wr", "Ws")] for k in range(2)]
    w3 = [l3(k) for k in ("Wq", "Wk", "Wv", "Wo")]
    ctx = ExitStack()
    shared = Shared(nc, ctx, w0)
    attention_pass(nc, "l0", x, kept[0], adj, (w0, None), float(D) ** -0.5,
                   True, True, l0("bv"), l0("bo"), None, 2.0, groups, shared, w1)
    attention_pass(nc, "l1", kept[0], kept[1], adj, (w1, (l1("bq"), l1("bk"))),
                   float(D // HEADS) ** -0.5, False, False, l1("bv"), None, l1("beta"), None, groups,
                   shared, w2[0])
    for k in range(2):
        digcn_pass(nc, f"l2{k}", kept[1 + k], kept[2 + k], adj, w2[k],
                   [l2(m)[k:k + 1, :] for m in ("bl", "br", "bs")], l2("ln_w")[k:k + 1, :], l2("ln_b")[k:k + 1, :],
                   kept[1] if k else None, groups, shared, w3 if k else w2[1])
    attention_pass(nc, "l3", kept[3], y, adj, (w3, None), float(D) ** -0.5,
                   True, True, l3("bv"), l3("bo"), None, 1.0, groups, shared, [])
    ctx.close()


_INS = (["x", "adj"] + [f"L0_gnn_{k}" for k in ("Wq", "Wk", "Wv", "bv", "Wo", "bo")]
        + [f"L1_gnn_{k}" for k in ("Wq", "bq", "Wk", "bk", "Wv", "bv", "beta")]
        + [f"L2_gnn_{k}" for k in ("Wl", "bl", "Ws", "bs", "Wr", "br", "ln_w", "ln_b")]
        + [f"L3_gnn_{k}" for k in ("Wq", "Wk", "Wv", "bv", "Wo", "bo")])


def kernel(**inputs):
    import numpy as np
    import concourse.bacc as bacc
    from concourse.bass_utils import run_bass_kernel_spmd

    nc = bacc.Bacc("TRN2", target_bir_lowering=False, num_devices=1)
    arrays, ins = {}, {}
    for name in _INS:
        a = np.ascontiguousarray(inputs[name])
        if a.ndim == 0:
            a = a.reshape(1)
        arrays[f"in_{name}"] = a
        ins[name] = nc.dram_tensor(f"in_{name}", a.shape, mybir.dt.from_np(a.dtype), kind="ExternalInput").ap()
    out = nc.dram_tensor("out", tuple(inputs["x"].shape), F32, kind="ExternalOutput").ap()
    graph_layers(nc, ins, out)
    return run_bass_kernel_spmd(nc, [arrays], core_ids=[0]).results[0]["out"]
```
